# Optimizing a Trainium2 kernel written in Bass

```python
import numpy as np
import jax
import jax.numpy as jnp

def _softmax(x, axis=-1):
    return jax.nn.softmax(x, axis=axis)

def _gelu(x):
    return jax.nn.gelu(x, approximate=True)

def _silu(x):
    return jax.nn.silu(x)

def _sigmoid(x):
    return jax.nn.sigmoid(x)

def _layernorm(x, axis=-1, eps=1e-05):
    m = jnp.mean(x, axis=axis, keepdims=True)
    v = jnp.var(x, axis=axis, keepdims=True)
    return (x - m) / jnp.sqrt(v + eps)

def _scatter_add(tgt, idx, src, axis=0):
    return tgt.at[idx].add(src)

def _segment_sum(src, seg, n):
    return jax.ops.segment_sum(src, seg, n)
kernel_name = 'mk_prb_d2_jaxref_r8_b872c7'

def setup_inputs(seed: int=0):
    np.random.seed(seed)
    _w = jnp.asarray

    def _L0_attn_setup():
        import jax, jax.numpy as jnp
        import numpy as np
        HIDDEN = 128
        NUM_HEADS = 16
        HEAD = HIDDEN // NUM_HEADS
        LEFT = 64
        RIGHT = 8
        NUM_POS = LEFT + RIGHT + 1
        key = jax.random.key(seed)
        ks = jax.random.split(key, 10)
        s = 1.0 / np.sqrt(HIDDEN)
        return {'hidden_states': jax.random.normal(ks[0], (4, 256, HIDDEN), jnp.float32), 'Wq': jax.random.normal(ks[1], (HIDDEN, HIDDEN), jnp.float32) * s, 'bq': jax.random.normal(ks[2], (HIDDEN,), jnp.float32) * 0.01, 'Wk': jax.random.normal(ks[3], (HIDDEN, HIDDEN), jnp.float32) * s, 'bk': jax.random.normal(ks[4], (HIDDEN,), jnp.float32) * 0.01, 'Wv': jax.random.normal(ks[5], (HIDDEN, HIDDEN), jnp.float32) * s, 'bv': jax.random.normal(ks[6], (HIDDEN,), jnp.float32) * 0.01, 'Wo': jax.random.normal(ks[7], (HIDDEN, HIDDEN), jnp.float32) * s, 'bo': jax.random.normal(ks[8], (HIDDEN,), jnp.float32) * 0.01, 'dist_emb': jax.random.normal(ks[9], (NUM_POS, HEAD), jnp.float32)}
    _L0_attn_in = _L0_attn_setup()

    def _L0_ffn_setup():
        import jax, jax.numpy as jnp
        import numpy as np
        TOP_K = 2
        EPS = 1e-05

        def layer_norm(x, g, b):
            mu = jnp.mean(x, axis=-1, keepdims=True)
            var = jnp.mean(jnp.square(x - mu), axis=-1, keepdims=True)
            return (x - mu) * jax.lax.rsqrt(var + EPS) * g + b
        key = jax.random.key(seed)
        ks = jax.random.split(key, 12)
        B, S, D, F, E = (2, 256, 128, 512, 8)
        std = 0.02
        return {'x': jax.random.normal(ks[0], (B, S, D), jnp.float32), 'g1': jnp.ones((D,), jnp.float32), 'be1': jnp.zeros((D,), jnp.float32), 'mix_w': jax.random.normal(ks[1], (D, D), jnp.float32) * std, 'mix_b': jnp.zeros((D,), jnp.float32), 'g2': jnp.ones((D,), jnp.float32), 'be2': jnp.zeros((D,), jnp.float32), 'router_w': jax.random.normal(ks[2], (D, E), jnp.float32) * std, 'w1': jax.random.normal(ks[3], (E, D, F), jnp.float32) * std, 'b1': jnp.zeros((E, F), jnp.float32), 'w2': jax.random.normal(ks[4], (E, F, D), jnp.float32) * std, 'b2': jnp.zeros((E, D), jnp.float32)}
    _L0_ffn_in = _L0_ffn_setup()

    def _L1_attn_setup():
        import jax, jax.numpy as jnp
        import numpy as np
        HIDDEN = 128
        HEADS = 16
        HEAD_DIM = HIDDEN // HEADS
        SCALE = HEAD_DIM ** (-0.5)
        key = jax.random.key(seed)
        ks = jax.random.split(key, 9)
        init = 1.0 / np.sqrt(HIDDEN)
        hidden_states = jax.random.normal(ks[0], (8, 128, HIDDEN), dtype=jnp.float32)

        def lin(k):
            kw, kb = jax.random.split(k)
            W = jax.random.uniform(kw, (HIDDEN, HIDDEN), jnp.float32, -init, init)
            b = jax.random.uniform(kb, (HIDDEN,), jnp.float32, -init, init)
            return (W, b)
        Wq, bq = lin(ks[1])
        Wk, bk = lin(ks[2])
        Wv, bv = lin(ks[3])
        Wo, bo = lin(ks[4])
        return {'hidden_states': hidden_states, 'Wq': Wq, 'bq': bq, 'Wk': Wk, 'bk': bk, 'Wv': Wv, 'bv': bv, 'Wo': Wo, 'bo': bo}
    _L1_attn_in = _L1_attn_setup()

    def _L1_ffn_setup():
        import jax, jax.numpy as jnp
        import numpy as np
        B, S, D, H, F, E = (2, 128, 128, 16, 512, 8)
        HD = D // H
        EPS = 1e-06

        def _layernorm(x, g, b):
            m = jnp.mean(x, axis=-1, keepdims=True)
            v = jnp.var(x, axis=-1, keepdims=True)
            return (x - m) / jnp.sqrt(v + EPS) * g + b
        key = jax.random.key(seed)
        ks = jax.random.split(key, 10)
        sc = 0.02
        x = jax.random.normal(ks[0], (B, S, D), jnp.float32)
        Wq = jax.random.normal(ks[1], (D, D), jnp.float32) * sc
        Wk = jax.random.normal(ks[2], (D, D), jnp.float32) * sc
        Wv = jax.random.normal(ks[3], (D, D), jnp.float32) * sc
        Wo = jax.random.normal(ks[4], (D, D), jnp.float32) * sc
        bo = jnp.zeros((D,), jnp.float32)
        Wr = jax.random.normal(ks[5], (D, E), jnp.float32) * sc
        We1 = jax.random.normal(ks[6], (E, D, F), jnp.float32) * sc
        be1 = jnp.zeros((E, F), jnp.float32)
        We2 = jax.random.normal(ks[7], (E, F, D), jnp.float32) * sc
        be2 = jnp.zeros((E, D), jnp.float32)
        ln1_g = jnp.ones((D,), jnp.float32)
        ln1_b = jnp.zeros((D,), jnp.float32)
        ln2_g = jnp.ones((D,), jnp.float32)
        ln2_b = jnp.zeros((D,), jnp.float32)
        return {'x': x, 'Wq': Wq, 'Wk': Wk, 'Wv': Wv, 'Wo': Wo, 'bo': bo, 'Wr': Wr, 'We1': We1, 'be1': be1, 'We2': We2, 'be2': be2, 'ln1_g': ln1_g, 'ln1_b': ln1_b, 'ln2_g': ln2_g, 'ln2_b': ln2_b}
    _L1_ffn_in = _L1_ffn_setup()
    _d = {'L0_attn_hidden_states': _L0_attn_in['hidden_states'], 'L0_attn_Wq': _L0_attn_in['Wq'], 'L0_attn_bq': _L0_attn_in['bq'], 'L0_attn_Wk': _L0_attn_in['Wk'], 'L0_attn_bk': _L0_attn_in['bk'], 'L0_attn_Wv': _L0_attn_in['Wv'], 'L0_attn_bv': _L0_attn_in['bv'], 'L0_attn_Wo': _L0_attn_in['Wo'], 'L0_attn_bo': _L0_attn_in['bo'], 'L0_attn_dist_emb': _L0_attn_in['dist_emb'], 'L0_ffn_g1': _L0_ffn_in['g1'], 'L0_ffn_be1': _L0_ffn_in['be1'], 'L0_ffn_mix_w': _L0_ffn_in['mix_w'], 'L0_ffn_mix_b': _L0_ffn_in['mix_b'], 'L0_ffn_g2': _L0_ffn_in['g2'], 'L0_ffn_be2': _L0_ffn_in['be2'], 'L0_ffn_router_w': _L0_ffn_in['router_w'], 'L0_ffn_w1': _L0_ffn_in['w1'], 'L0_ffn_b1': _L0_ffn_in['b1'], 'L0_ffn_w2': _L0_ffn_in['w2'], 'L0_ffn_b2': _L0_ffn_in['b2'], 'L1_attn_Wq': _L1_attn_in['Wq'], 'L1_attn_bq': _L1_attn_in['bq'], 'L1_attn_Wk': _L1_attn_in['Wk'], 'L1_attn_bk': _L1_attn_in['bk'], 'L1_attn_Wv': _L1_attn_in['Wv'], 'L1_attn_bv': _L1_attn_in['bv'], 'L1_attn_Wo': _L1_attn_in['Wo'], 'L1_attn_bo': _L1_attn_in['bo'], 'L1_ffn_Wq': _L1_ffn_in['Wq'], 'L1_ffn_Wk': _L1_ffn_in['Wk'], 'L1_ffn_Wv': _L1_ffn_in['Wv'], 'L1_ffn_Wo': _L1_ffn_in['Wo'], 'L1_ffn_bo': _L1_ffn_in['bo'], 'L1_ffn_Wr': _L1_ffn_in['Wr'], 'L1_ffn_We1': _L1_ffn_in['We1'], 'L1_ffn_be1': _L1_ffn_in['be1'], 'L1_ffn_We2': _L1_ffn_in['We2'], 'L1_ffn_be2': _L1_ffn_in['be2'], 'L1_ffn_ln1_g': _L1_ffn_in['ln1_g'], 'L1_ffn_ln1_b': _L1_ffn_in['ln1_b'], 'L1_ffn_ln2_g': _L1_ffn_in['ln2_g'], 'L1_ffn_ln2_b': _L1_ffn_in['ln2_b']}
    _x0 = _d['L0_attn_hidden_states']
    _d['L0_attn_hidden_states'] = jax.random.normal(jax.random.fold_in(jax.random.key(seed), 1), (16, 256, 128), dtype=_x0.dtype)
    del _x0
    return _d

def reference(L0_attn_hidden_states, L0_attn_Wq, L0_attn_bq, L0_attn_Wk, L0_attn_bk, L0_attn_Wv, L0_attn_bv, L0_attn_Wo, L0_attn_bo, L0_attn_dist_emb, L0_ffn_g1, L0_ffn_be1, L0_ffn_mix_w, L0_ffn_mix_b, L0_ffn_g2, L0_ffn_be2, L0_ffn_router_w, L0_ffn_w1, L0_ffn_b1, L0_ffn_w2, L0_ffn_b2, L1_attn_Wq, L1_attn_bq, L1_attn_Wk, L1_attn_bk, L1_attn_Wv, L1_attn_bv, L1_attn_Wo, L1_attn_bo, L1_ffn_Wq, L1_ffn_Wk, L1_ffn_Wv, L1_ffn_Wo, L1_ffn_bo, L1_ffn_Wr, L1_ffn_We1, L1_ffn_be1, L1_ffn_We2, L1_ffn_be2, L1_ffn_ln1_g, L1_ffn_ln1_b, L1_ffn_ln2_g, L1_ffn_ln2_b):

    def _L0_attn_ref(hidden_states, Wq, bq, Wk, bk, Wv, bv, Wo, bo, dist_emb):
        import jax, jax.numpy as jnp
        import numpy as np
        HIDDEN = 128
        NUM_HEADS = 16
        HEAD = HIDDEN // NUM_HEADS
        LEFT = 64
        RIGHT = 8
        NUM_POS = LEFT + RIGHT + 1
        B, L, H = hidden_states.shape
        scale = 1.0 / np.sqrt(HEAD)

        def proj(W, b):
            return (hidden_states @ W.T + b).reshape(B, L, NUM_HEADS, HEAD).transpose(0, 2, 1, 3)
        q = proj(Wq, bq)
        k = proj(Wk, bk)
        v = proj(Wv, bv)
        attn = jnp.einsum('bhld,bhrd->bhlr', q, k) * scale
        dist = jnp.arange(L)[None, :] - jnp.arange(L)[:, None]
        dist = jnp.clip(dist, -LEFT, RIGHT) + LEFT
        pos_emb = dist_emb[dist]
        rel = jnp.einsum('bhld,lrd->bhlr', q, pos_emb) * scale
        attn = jax.nn.softmax(attn + rel, axis=-1)
        out = jnp.einsum('bhlr,bhrd->bhld', attn, v)
        out = out.transpose(0, 2, 1, 3).reshape(B, L, H)
        return out @ Wo.T + bo

    def _L0_ffn_ref(x, g1, be1, mix_w, mix_b, g2, be2, router_w, w1, b1, w2, b2):
        import jax, jax.numpy as jnp
        import numpy as np
        TOP_K = 2
        EPS = 1e-05

        def layer_norm(x, g, b):
            mu = jnp.mean(x, axis=-1, keepdims=True)
            var = jnp.mean(jnp.square(x - mu), axis=-1, keepdims=True)
            return (x - mu) * jax.lax.rsqrt(var + EPS) * g + b
        res = x
        n = layer_norm(x, g1, be1)
        x = res + n + (n @ mix_w + mix_b)
        res = x
        n = layer_norm(x, g2, be2)
        B, S, D = n.shape
        E = w1.shape[0]
        flat = n.reshape(-1, D)
        probs = jax.nn.softmax(flat @ router_w, axis=-1)
        topw, topi = jax.lax.top_k(probs, TOP_K)
        combine = jnp.sum(jax.nn.one_hot(topi, E, dtype=flat.dtype) * topw[..., None], axis=1)
        h = jax.nn.silu(jnp.einsum('td,edf->tef', flat, w1) + b1)
        y = jnp.einsum('tef,efd->ted', h, w2) + b2
        out = jnp.einsum('te,ted->td', combine, y)
        return res + out.reshape(B, S, D)

    def _L1_attn_ref(hidden_states, Wq, bq, Wk, bk, Wv, bv, Wo, bo):
        import jax, jax.numpy as jnp
        import numpy as np
        HIDDEN = 128
        HEADS = 16
        HEAD_DIM = HIDDEN // HEADS
        SCALE = HEAD_DIM ** (-0.5)
        b, s, d = hidden_states.shape
        q = (hidden_states @ Wq.T + bq).reshape(b, s, HEADS, HEAD_DIM)
        k = (hidden_states @ Wk.T + bk).reshape(b, s, HEADS, HEAD_DIM)
        v = (hidden_states @ Wv.T + bv).reshape(b, s, HEADS, HEAD_DIM)
        q = q * SCALE
        scores = jnp.einsum('bqhd,bkhd->bhqk', q, k)
        probs = jax.nn.softmax(scores.astype(jnp.float32), axis=-1).astype(scores.dtype)
        out = jnp.einsum('bhqk,bkhd->bqhd', probs, v).reshape(b, s, d)
        return out @ Wo.T + bo

    def _L1_ffn_ref(x, Wq, Wk, Wv, Wo, bo, Wr, We1, be1, We2, be2, ln1_g, ln1_b, ln2_g, ln2_b):
        import jax, jax.numpy as jnp
        import numpy as np
        B, S, D, H, F, E = (2, 128, 128, 16, 512, 8)
        HD = D // H
        EPS = 1e-06

        def _layernorm(x, g, b):
            m = jnp.mean(x, axis=-1, keepdims=True)
            v = jnp.var(x, axis=-1, keepdims=True)
            return (x - m) / jnp.sqrt(v + EPS) * g + b
        b, s, d = x.shape

        def split_heads(t):
            return t.reshape(b, s, H, HD).transpose(0, 2, 1, 3)
        q = split_heads(x @ Wq)
        k = split_heads(x @ Wk)
        v = split_heads(x @ Wv)
        scores = jnp.einsum('bhqd,bhkd->bhqk', q, k) / jnp.sqrt(jnp.float32(HD))
        attn_w = jax.nn.softmax(scores, axis=-1)
        ctx = jnp.einsum('bhqk,bhkd->bhqd', attn_w, v)
        ctx = ctx.transpose(0, 2, 1, 3).reshape(b, s, d)
        attn_out = ctx @ Wo + bo
        out1 = _layernorm(x + attn_out, ln1_g, ln1_b)
        router_probs = jax.nn.softmax(out1 @ Wr, axis=-1)
        top_g, top_i = jax.lax.top_k(router_probs, 2)
        top_g = jax.nn.softmax(top_g, axis=-1)
        acc = jnp.zeros_like(out1)
        for e in range(E):
            sel = top_i == e
            msk = jnp.any(sel, axis=-1)[..., None].astype(out1.dtype)
            h = jax.nn.gelu(out1 * msk @ We1[e] + be1[e], approximate=False)
            o = h @ We2[e] + be2[e]
            gate = jnp.sum(top_g * sel.astype(top_g.dtype), axis=-1, keepdims=True)
            acc = acc + o * gate
        return _layernorm(out1 + acc, ln2_g, ln2_b)
    x = L0_attn_hidden_states
    xn = _layernorm(x, axis=-1)
    x = x + _L0_attn_ref(xn, L0_attn_Wq, L0_attn_bq, L0_attn_Wk, L0_attn_bk, L0_attn_Wv, L0_attn_bv, L0_attn_Wo, L0_attn_bo, L0_attn_dist_emb) + _L0_ffn_ref(xn, L0_ffn_g1, L0_ffn_be1, L0_ffn_mix_w, L0_ffn_mix_b, L0_ffn_g2, L0_ffn_be2, L0_ffn_router_w, L0_ffn_w1, L0_ffn_b1, L0_ffn_w2, L0_ffn_b2)
    xn = _layernorm(x, axis=-1)
    x = x + _L1_attn_ref(xn, L1_attn_Wq, L1_attn_bq, L1_attn_Wk, L1_attn_bk, L1_attn_Wv, L1_attn_bv, L1_attn_Wo, L1_attn_bo) + _L1_ffn_ref(xn, L1_ffn_Wq, L1_ffn_Wk, L1_ffn_Wv, L1_ffn_Wo, L1_ffn_bo, L1_ffn_Wr, L1_ffn_We1, L1_ffn_be1, L1_ffn_We2, L1_ffn_be2, L1_ffn_ln1_g, L1_ffn_ln1_b, L1_ffn_ln2_g, L1_ffn_ln2_b)
    return x

_drawn_inputs = setup_inputs


def setup_inputs(seed=0):
    import zlib

    import numpy as np

    out = dict(_drawn_inputs(seed))
    spreads = {'L0_ffn_g1': (1.0, 0.2),
     'L0_ffn_be1': (0.0, 0.1),
     'L0_ffn_mix_b': (0.0, 0.1),
     'L0_ffn_g2': (1.0, 0.6),
     'L0_ffn_be2': (0.0, 0.8),
     'L0_ffn_b1': (0.0, 0.8),
     'L0_ffn_b2': (0.0, 0.8),
     'L1_ffn_bo': (0.0, 0.338),
     'L1_ffn_be1': (0.0, 0.8),
     'L1_ffn_be2': (0.0, 2.0),
     'L1_ffn_ln1_g': (1.0, 0.58),
     'L1_ffn_ln1_b': (0.0, 0.3),
     'L1_ffn_ln2_g': (1.0, 0.6),
     'L1_ffn_ln2_b': (0.0, 1.104)}
    factors = {'L0_attn_bq': 33.819,
     'L0_attn_bk': 64.0,
     'L0_attn_bv': 8.0,
     'L0_attn_bo': 8.0,
     'L0_ffn_router_w': 7.554,
     'L0_ffn_w1': 8.0,
     'L0_ffn_w2': 8.0,
     'L1_attn_Wq': 8.0,
     'L1_attn_bq': 8.0,
     'L1_attn_Wk': 8.0,
     'L1_attn_bk': 64.0,
     'L1_attn_Wv': 7.91,
     'L1_attn_bv': 6.78,
     'L1_attn_Wo': 5.455,
     'L1_attn_bo': 16.231,
     'L1_ffn_Wq': 8.0,
     'L1_ffn_Wk': 8.0,
     'L1_ffn_Wv': 8.0,
     'L1_ffn_Wo': 8.0,
     'L1_ffn_Wr': 3.221,
     'L1_ffn_We1': 5.968,
     'L1_ffn_We2': 5.396}
    for name, (base, spread) in spreads.items():
        noise = np.random.default_rng([zlib.crc32(name.encode()), seed]).standard_normal(out[name].shape)
        drawn = base * np.exp(spread * noise) if base else spread * noise
        out[name] = jnp.asarray(drawn.astype(out[name].dtype))
    for name, factor in factors.items():
        out[name] = (out[name] * factor).astype(out[name].dtype)
    return out
```

```python
from contextlib import ExitStack

import concourse.bass as bass
from concourse import mybir

B, L, D = 16, 256, 128
P = 128
T = L // P
HEADS, HD = 16, 8
LEFT, RIGHT = 64, 8
NPOS = LEFT + RIGHT + 1
E, F = 8, 512
FT = F // P
G, GH = 4, 4
UNITS = G * T
RHO = P // HD
ROWS = ["L0_attn_bv", "L0_attn_bo", "L0_ffn_g1", "L0_ffn_be1", "L0_ffn_mix_b", "L0_ffn_g2", "L0_ffn_be2",
        "L1_attn_bv", "L1_attn_bo", "L1_ffn_bo", "L1_ffn_ln1_g", "L1_ffn_ln1_b", "L1_ffn_ln2_g", "L1_ffn_ln2_b"]
ATTN = ["L0_attn", "L1_attn", "L1_ffn"]
EYE, RMASK, HMASK, EYE16, LOWER = 0, 128, 384, 388, 404
NCONST = LOWER + E * E


class Signal:

    def __init__(self, sem, layer0, layer1):
        self.sem, self.counts = sem, (layer0, layer1)

    def at(self, layer, i, k):
        if layer == 0:
            return i * self.counts[0] + k
        return i * self.counts[1] + (B * self.counts[0] + k)


def build(nc, a, out, scratch=None):
    f32, f32r = mybir.dt.float32, mybir.dt.float32r
    ALU, ACT, AX = mybir.AluOpType, mybir.ActivationFunctionType, mybir.AxisListType
    SCALE = float(HD) ** -0.5
    ctx = ExitStack()
    with ctx:
        def sb(name, shape, dt=f32):
            return ctx.enter_context(nc.sbuf_tensor(name, shape, dt))

        def signal(name, layer0, layer1):
            return Signal(ctx.enter_context(nc.semaphore(name)), layer0, layer1)

        X = sb("X", [P, B * T, D])
        const = sb("const", [P, NCONST])
        rows = sb("rows", [P, len(ROWS), D])
        eye = const[:, EYE:EYE + P]
        rmask = const[:, RMASK:RMASK + L]
        wq = sb("wq", [P, 3, G, P])
        wk = sb("wk", [P, 3, G, P])
        wv = sb("wv", [P, 3, D])
        wo = sb("wo", [P, 3, D])
        wqx = sb("wqx", [P, HEADS, RHO, HD])
        bq = sb("bq", [P, 2, G])
        bk = sb("bk", [P, 2, G])
        bqx = sb("bqx", [P, HEADS])
        mixw = sb("mixw", [P, D])
        rw = sb("rw", [P, 2, E])
        w1 = sb("w1", [P, 2, E, F])
        w2 = sb("w2", [P, 2, E, FT, D])
        b1 = sb("b1", [P, 2, E, FT])
        b2 = sb("b2", [E, 2, D])
        ext = sb("ext", [HD, 512])
        toep = sb("toep", [P, 496])
        ones16 = sb("ones16", [RHO, P], f32r)
        half = sb("half", [P, T])

        xn = sb("xn", [P, T, D])
        stats = sb("stats", [P, T, 6])
        mv = sb("mv", [P, T, 2])
        ve = sb("ve", [P, T])
        rstd = sb("rstd", [P, T])
        xT = sb("xT", [P, L])
        qf = sb("qf", [P, G, L])
        kf = sb("kf", [P, G, L])
        qs = sb("qs", [P, G, L], f32r)
        ks = sb("ks", [P, G, L], f32r)
        qm = sb("qm", [P, G, GH, L], f32r)
        qx = sb("qx", [P, HEADS, L])
        vp = sb("vp", [P, T, HEADS, 32])
        pm = sb("pm", [P, 32])
        pm2 = sb("pm2", [P, 16])
        nm = sb("nm", [16, 32])
        shift = sb("shift", [16, 16, 32], f32r)
        probs = sb("probs", [P, 2, T, GH * P])
        pv = sb("pv", [P, P])
        rden = sb("rden", [P, GH])
        ao = sb("ao", [P, T, D])
        aoT = sb("aoT", [P, L])
        n1 = sb("n1", [P, T, D])
        x1 = sb("x1", [P, T, D])
        res = sb("res", [P, T, D])
        hT = sb("hT", [P, 2, FT, L])
        logit = sb("logit", [P, T, E])
        prob = sb("prob", [P, T, E])
        red = sb("red", [P, T])
        red2 = sb("red2", [P, T])
        cmp = sb("cmp", [P, T, E, E])
        cmp2 = sb("cmp2", [P, T, E, E])
        sel = sb("sel", [P, T, E])
        gate = sb("gate", [P, T, E])
        gT = sb("gT", [E, L])

        PS = [ctx.enter_context(nc.psum_tensor(f"bank{n}", [P, 1024], f32)) for n in range(2)] + \
             [ctx.enter_context(nc.psum_tensor(f"bank{n}", [P, 512], f32)) for n in range(4, 8)]
        score = PS[0:2]
        p4, p5, p6, p7 = PS[2:]

        loaded = ctx.enter_context(nc.semaphore("loaded"))
        shifts_loaded = ctx.enter_context(nc.semaphore("shifts_loaded"))
        stored = ctx.enter_context(nc.semaphore("stored"))
        ext_ready = ctx.enter_context(nc.semaphore("ext_ready"))
        ready = ctx.enter_context(nc.semaphore("ready"))
        dve = signal("dve", 0, 0)
        var_ready = signal("var_ready", 3, 3)
        rstd_ready = signal("rstd_ready", 3, 3)
        rows_in = signal("rows_in", 3, 2)
        turned = signal("turned", 4, 4)
        turned_out = signal("turned_out", 4, 4)
        q_proj = signal("q_proj", 1, 2)
        k_proj = signal("k_proj", 1, 2)
        v_proj = signal("v_proj", 1, 2)
        q_split = signal("q_split", 1, 2)
        k_split = signal("k_split", 1, 2)
        v_ready = signal("v_ready", 1, 2)
        q_masked = signal("q_masked", G, 2 * G)
        qx_proj = signal("qx_proj", HEADS // 2, 0)
        qx_out = signal("qx_out", HEADS // 2, 0)
        scores_ready = signal("scores_ready", UNITS, 2 * UNITS)
        part_max = signal("part_max", UNITS, 2 * UNITS)
        max_turned = signal("max_turned", UNITS, 2 * UNITS)
        nm_ready = signal("nm_ready", UNITS, 2 * UNITS)
        shift_rows = signal("shift_rows", UNITS, 2 * UNITS)
        shifted = signal("shifted", UNITS, 2 * UNITS)
        probs_ready = signal("probs_ready", UNITS, 2 * UNITS)
        pv_done = signal("pv_done", UNITS, 2 * UNITS)
        pv_out = signal("pv_out", UNITS, 2 * UNITS)
        pv_turned = signal("pv_turned", UNITS, 2 * UNITS)
        divided = signal("divided", UNITS, 2 * UNITS)
        o_proj = signal("o_proj", 1, 2)
        o_added = signal("o_added", 1, 2)
        mix_done = signal("mix_done", 1, 0)
        logits_done = signal("logits_done", 1, 1)
        centred = signal("centred", 1, 2)
        exps_done = signal("exps_done", 1, 2)
        gates_ready = signal("gates_ready", 1, 1)
        gates_turned = signal("gates_turned", 1, 1)
        gates_out = signal("gates_out", 1, 1)
        b2_done = signal("b2_done", 1, 1)
        b2_added = signal("b2_added", 1, 1)
        up_done = signal("up_done", 2 * E, 2 * E)
        act_done = signal("act_done", 2 * E, 2 * E)
        down_done = signal("down_done", E, E)
        acc_done = signal("acc_done", E, E)
        out_ready = signal("out_ready", 0, 1)

        def row(name):
            return rows[:, ROWS.index(name), :].unsqueeze(1).broadcast_to((P, T, D))

        N_LOADS = [0]
        block = ctx.enter_context(nc.Block())

        @block.sync
        def _(sp):
            def load(dst, src):
                sp.dma_start(dst, src).then_inc(loaded, 16)
                N_LOADS[0] += 1

            x = a["L0_attn_hidden_states"].rearrange("b (t p) d -> p (b t) d", p=P)
            sp.dma_start(ext[:, 192:192 + NPOS], a["L0_attn_dist_emb"]).then_inc(shifts_loaded, 16)
            load(const[:, :], a["const"])
            load(X[:, :, :], x)
            load(rows[:, :, :], a["rows"].partition_broadcast(P))
            for n, name in enumerate(ATTN):
                for w, key in ((wq, "Wq"), (wk, "Wk")):
                    src = a[f"{name}_{key}"].rearrange("p (g c) -> p g c", g=G)
                    for copy in range(4):
                        load(w[:, n, :, 32 * copy:32 * copy + 32], src)
                load(wv[:, n, :], a[f"{name}_Wv"])
                load(wo[:, n, :], a[f"{name}_Wo"])
                if n < 2:
                    for b, key in ((bq, "bq"), (bk, "bk")):
                        for copy in range(4):
                            load(b[32 * copy:32 * copy + 32, n, :], a[f"{name}_{key}"])
            for r in range(RHO):
                load(wqx[:, :, r, :], a["L0_attn_Wq"].rearrange("p (h d) -> p h d", d=HD))
                load(bqx[HD * r:HD * r + HD, :], a["bq_heads"])
            load(mixw[:, :], a["L0_ffn_mix_w"])
            for n, (r, u, bu, dn, bd) in enumerate((("router_w", "w1", "b1", "w2", "b2"), ("Wr", "We1", "be1", "We2", "be2"))):
                load(rw[:, n, :], a[f"L{n}_ffn_{r}"])
                load(w1[:, n, :, :], a[f"L{n}_ffn_{u}"].rearrange("e p f -> p e f"))
                load(w2[:, n, :, :, :].rearrange("p e t d -> p (e t) d"), a[f"L{n}_ffn_{dn}"].rearrange("e (t p) d -> p (e t) d", p=P))
                load(b1[:, n, :, :].rearrange("p e t -> p (e t)"), a[f"L{n}_ffn_{bu}"])
                load(b2[:, n, :], a[f"L{n}_ffn_{bd}"])
            sp.wait_ge(ext_ready, 2)
            for r in range(RHO):
                sp.dma_start(toep[HD * r:HD * r + HD, :], ext[:, 16 - r:16 - r + 496]).then_inc(shifts_loaded, 16)
            y = out.rearrange("b (t p) d -> b p t d", p=P)
            with sp.Fori(0, B) as i:
                sp.wait_ge(out_ready.sem, out_ready.at(1, i, 1))
                sp.dma_start(y[bass.ds(i, 1)].rearrange("b p t d -> p (b t) d"), X[:, bass.ds(i * T, T), :]).then_inc(stored, 16)
            sp.wait_ge(stored, 16 * B)

        @block.gpsimd
        def _(pool):
            pool.memset(half[:, :], -0.5).then_inc(ready, 1)
            pool.memset(ones16[:, :].bitcast(f32), 1.0).then_inc(ready, 1)
            pool.memset(vp[:, :, :, :], 0.0).then_inc(ready, 1)
            pool.wait_ge(ready, 3)
            pool.memset(vp[:, :, :, HD:HD + 1], 1.0).then_inc(ready, 1)
            pool.wait_ge(ready, 4)
            pool.wait_ge(loaded, 16 * N_LOADS[0])

            def root(layer, i, k):
                pool.wait_ge(var_ready.sem, var_ready.at(layer, i, k))
                pool.tensor_tensor(rstd[:, :], ve[:, :], half[:, :], ALU.pow).then_inc(rstd_ready.sem, 1)

            def attend(layer, i, n):
                pool.wait_ge(q_split.sem, q_split.at(layer, i, n + 1))
                for g in range(G):
                    pool.tensor_tensor(qm[0:96, g, :, :], qs[0:96, g, :].bitcast(f32).unsqueeze(1).broadcast_to((96, GH, L)),
                                       const[0:96, HMASK:HMASK + GH].unsqueeze(2).broadcast_to((96, GH, L)),
                                       ALU.mult).then_inc(q_masked.sem, 1)
                for u in range(UNITS):
                    pool.wait_ge(nm_ready.sem, nm_ready.at(layer, i, n * UNITS + u + 1))
                    pool.tensor_tensor(shift[:, :, :], nm[:, :].unsqueeze(1).broadcast_to((16, 16, 32)),
                                       const[0:16, EYE16:EYE16 + 16].unsqueeze(2).broadcast_to((16, 16, 32)),
                                       ALU.mult).then_inc(shift_rows.sem, 1)

            with pool.Fori(0, B) as i:
                root(0, i, 1)
                attend(0, i, 0)
                root(0, i, 2)
                root(0, i, 3)
            with pool.Fori(0, B) as i:
                root(1, i, 1)
                attend(1, i, 0)
                root(1, i, 2)
                attend(1, i, 1)
                root(1, i, 3)

        @block.scalar
        def _(act):
            act.wait_ge(loaded, 16 * N_LOADS[0])

            def turn_out(layer, i, k, dst, rows_=P):
                act.wait_ge(turned.sem, turned.at(layer, i, k))
                act.activation(dst, p6[0:rows_, 0:L], ACT.Copy).then_inc(turned_out.sem, 1)

            def attend(layer, i, n):
                for u in range(UNITS):
                    k = n * UNITS + u + 1
                    act.wait_ge(shifted.sem, shifted.at(layer, i, k))
                    act.activation(probs[:, u % 2, :, :].rearrange("p t c -> p (t c)"), score[u % 2][:, :], ACT.Exp,
                                   scale=SCALE).then_inc(probs_ready.sem, 1)
                    act.wait_ge(pv_done.sem, pv_done.at(layer, i, k))
                    act.activation(pv[:, :], p6[:, 0:P], ACT.Copy).then_inc(pv_out.sem, 1)

            def experts(layer, i, func):
                act.wait_ge(gates_turned.sem, gates_turned.at(layer, i, 1))
                act.activation(gT[:, :], p6[0:E, 0:L], ACT.Copy).then_inc(gates_out.sem, 1)
                for e in range(E):
                    for pair in range(2):
                        act.wait_ge(up_done.sem, up_done.at(layer, i, 2 * e + pair + 1))
                        for ft in (2 * pair, 2 * pair + 1):
                            last = act.activation(hT[:, e % 2, ft, :], (p4, p5)[pair][:, (ft % 2) * L:(ft % 2 + 1) * L], func,
                                                  bias=b1[:, layer, e, ft:ft + 1])
                        last.then_inc(act_done.sem, 1)

            def centre_exp(layer, i, k, dst):
                act.wait_ge(centred.sem, centred.at(layer, i, k))
                act.activation(dst, logit[:, :, :], ACT.Exp).then_inc(exps_done.sem, 1)

            with act.Fori(0, B) as i:
                turn_out(0, i, 1, xT[:, :])
                attend(0, i, 0)
                turn_out(0, i, 2, aoT[:, :])
                turn_out(0, i, 3, xT[:, :])
                turn_out(0, i, 4, xT[:, :])
                centre_exp(0, i, 1, prob[:, :, :])
                experts(0, i, ACT.Silu)
            with act.Fori(0, B) as i:
                turn_out(1, i, 1, xT[:, :])
                attend(1, i, 0)
                turn_out(1, i, 2, aoT[:, :])
                attend(1, i, 1)
                turn_out(1, i, 3, aoT[:, :])
                turn_out(1, i, 4, xT[:, :])
                centre_exp(1, i, 1, prob[:, :, :])
                centre_exp(1, i, 2, gate[:, :, :])
                experts(1, i, ACT.Gelu)

        @block.tensor
        def _(pe):
            pe.wait_ge(loaded, 16 * N_LOADS[0])
            pe.wait_ge(ready, 4)
            pe.wait_ge(shifts_loaded, 16 * (1 + RHO))

            def turn(layer, i, k, src, written, n):
                pe.wait_ge(written.sem, written.at(layer, i, n))
                for t in range(T):
                    last = pe.transpose(p6[:, t * P:(t + 1) * P], src[:, t, :], eye)
                last.then_inc(turned.sem, 1)
                pe.wait_ge(turned_out.sem, turned_out.at(layer, i, k))

            def by_token(dst, lhs, w):
                c = w.shape[-1]
                for t in range(T):
                    last = pe.matmul(dst[:, t * c:(t + 1) * c], lhs[:, t * P:(t + 1) * P], w, start=True, stop=True)
                return last

            def project(n):
                for w, buf, done in ((wq, score[0], q_proj), (wk, score[1], k_proj)):
                    for g in range(G):
                        last = pe.matmul(buf[:, g * L:(g + 1) * L], w[:, n, g, :], xT[:, :], start=True, stop=True)
                    last.then_inc(done.sem, 1)
                by_token(p7, xT, wv[:, n, :]).then_inc(v_proj.sem, 1)

            def attend(layer, i, n):
                def scores(u):
                    g, half_ = divmod(u, T)
                    if u >= 2:
                        pe.wait_ge(probs_ready.sem, probs_ready.at(layer, i, n * UNITS + u - 1))
                    pe.wait_ge(q_masked.sem, q_masked.at(layer, i, n * G + g + 1))
                    for kb in range(T):
                        dst = score[u % 2][:, kb * 512:(kb + 1) * 512]
                        last = pe.matmul(dst, ks[0:96, g, kb * P:(kb + 1) * P], qm[0:96, g, :, half_ * P:(half_ + 1) * P],
                                         start=True, stop=layer == 1)
                        if layer == 0:
                            view = dst.rearrange("p (h l) -> p h l", h=GH)
                            for m in range(P // RHO):
                                at = kb * P - (half_ * P + m * RHO) + 240
                                l0 = half_ * P + m * RHO
                                last = pe.matmul(view[:, :, m * RHO:(m + 1) * RHO], toep[:, at:at + P],
                                                 qx[:, g * GH:(g + 1) * GH, l0:l0 + RHO],
                                                 start=False, stop=m == P // RHO - 1)
                    last.then_inc(scores_ready.sem, 1)

                def turn_max(u):
                    pe.wait_ge(part_max.sem, part_max.at(layer, i, n * UNITS + u + 1))
                    pe.transpose(p5[0:16, 0:P], pm2[:, :], eye).then_inc(max_turned.sem, 1)

                def subtract(u):
                    pe.wait_ge(shift_rows.sem, shift_rows.at(layer, i, n * UNITS + u + 1))
                    for kb in range(T):
                        last = pe.matmul(score[u % 2][:, kb * 512:(kb + 1) * 512], ones16[:, :],
                                         shift[:, :, :].rearrange("p a b -> p (a b)"), start=False, stop=True,
                                         skip_group_check=True)
                    last.then_inc(shifted.sem, 1)

                def values(u):
                    g = u // T
                    pe.wait_ge(probs_ready.sem, probs_ready.at(layer, i, n * UNITS + u + 1))
                    for kb in range(T):
                        for h in range(GH):
                            last = pe.matmul(p6[32 * h:32 * h + 32, 0:P], vp[:, kb, g * GH + h, :],
                                             probs[:, u % 2, kb, h * P:(h + 1) * P], start=kb == 0, stop=kb == T - 1)
                    last.then_inc(pv_done.sem, 1)
                    pe.wait_ge(pv_out.sem, pv_out.at(layer, i, n * UNITS + u + 1))
                    if u:
                        pe.wait_ge(divided.sem, divided.at(layer, i, n * UNITS + u))
                    pe.transpose(p7[:, 0:P], pv[:, :], eye).then_inc(pv_turned.sem, 1)

                pe.wait_ge(k_split.sem, k_split.at(layer, i, n + 1))
                pe.wait_ge(v_ready.sem, v_ready.at(layer, i, n + 1))
                scores(0)
                for u in range(UNITS):
                    if u + 1 < UNITS:
                        scores(u + 1)
                    turn_max(u)
                    if u:
                        values(u - 1)
                    subtract(u)
                values(UNITS - 1)

            def out_project(layer, i, n, k, which):
                turn(layer, i, k, ao, divided, (n + 1) * UNITS)
                by_token(p7, aoT, wo[:, which, :]).then_inc(o_proj.sem, 1)

            def experts(layer, i):
                pe.wait_ge(gates_ready.sem, gates_ready.at(layer, i, 1))
                for t in range(T):
                    last = pe.transpose(p6[0:E, t * P:(t + 1) * P], gate[:, t, :], eye)
                last.then_inc(gates_turned.sem, 1)
                pe.wait_ge(gates_out.sem, gates_out.at(layer, i, 1))
                by_token(p7, gT, b2[:, layer, :]).then_inc(b2_done.sem, 1)

                def up(e):
                    for pair in range(2):
                        if e:
                            pe.wait_ge(act_done.sem, act_done.at(layer, i, 2 * (e - 1) + pair + 1))
                        for ft in (2 * pair, 2 * pair + 1):
                            last = pe.matmul((p4, p5)[pair][:, (ft % 2) * L:(ft % 2 + 1) * L],
                                             w1[:, layer, e, ft * P:(ft + 1) * P], xT[:, :], start=True, stop=True)
                        last.then_inc(up_done.sem, 1)

                def down(e):
                    pe.wait_ge(act_done.sem, act_done.at(layer, i, 2 * e + 2))
                    if e:
                        pe.wait_ge(acc_done.sem, acc_done.at(layer, i, e))
                    else:
                        pe.wait_ge(b2_added.sem, b2_added.at(layer, i, 1))
                    for t in range(T):
                        for ft in range(FT):
                            last = pe.matmul(p7[:, t * D:(t + 1) * D], hT[:, e % 2, ft, t * P:(t + 1) * P],
                                             w2[:, layer, e, ft, :], start=ft == 0, stop=ft == FT - 1)
                    last.then_inc(down_done.sem, 1)

                up(0)
                for e in range(E):
                    if e + 1 < E:
                        up(e + 1)
                    down(e)

            with pe.Fori(0, B) as i:
                turn(0, i, 1, xn, rows_in, 1)
                project(0)
                for j in range(HEADS // 2):
                    if j >= 2:
                        pe.wait_ge(qx_out.sem, qx_out.at(0, i, j - 1))
                    for h in (2 * j, 2 * j + 1):
                        last = pe.matmul((p4, p5)[j % 2][:, (h % 2) * L:(h % 2 + 1) * L],
                                         wqx[:, h, :, :].rearrange("p r d -> p (r d)"), xT[:, :], start=True, stop=True)
                    last.then_inc(qx_proj.sem, 1)
                pe.wait_ge(qx_out.sem, qx_out.at(0, i, HEADS // 2))
                attend(0, i, 0)
                out_project(0, i, 0, 2, 0)
                turn(0, i, 3, n1, rows_in, 2)
                pe.wait_ge(o_added.sem, o_added.at(0, i, 1))
                by_token(p7, xT, mixw[:, :]).then_inc(mix_done.sem, 1)
                turn(0, i, 4, n1, rows_in, 3)
                by_token(p7, xT, rw[:, 0, :]).then_inc(logits_done.sem, 1)
                experts(0, i)
            with pe.Fori(0, B) as i:
                turn(1, i, 1, xn, rows_in, 1)
                project(2)
                attend(1, i, 0)
                out_project(1, i, 0, 2, 2)
                pe.wait_ge(o_added.sem, o_added.at(1, i, 1))
                project(1)
                attend(1, i, 1)
                out_project(1, i, 1, 3, 1)
                pe.wait_ge(o_added.sem, o_added.at(1, i, 2))
                turn(1, i, 4, n1, rows_in, 2)
                by_token(p7, xT, rw[:, 1, :]).then_inc(logits_done.sem, 1)
                experts(1, i)

        @block.vector
        def _(v):
            v.wait_ge(shifts_loaded, 16)
            v.memset(ext[:, 0:192], 0.0)
            v.memset(ext[:, 192 + NPOS:512], 0.0).then_inc(dve.sem, 1)
            v.wait_ge(dve.sem, 1)
            v.tensor_scalar(ext[:, 0:192], ext[:, 0:192], ext[:, 192:193], None, ALU.add).then_inc(ext_ready, 1)
            v.tensor_scalar(ext[:, 192 + NPOS:512], ext[:, 192 + NPOS:512], ext[:, 191 + NPOS:192 + NPOS], None,
                            ALU.add).then_inc(ext_ready, 1)
            v.wait_ge(loaded, 16 * N_LOADS[0])
            v.wait_ge(ready, 4)

            chain_len = {}
            state = {}

            def link(ins):
                state["n"] += 1
                ins.then_inc(dve.sem, 1)
                v.wait_ge(dve.sem, state["base"] + state["n"])

            def norm(layer, i, k, src, dst, eps, gain=None, add=None, signal_=None):
                for t in range(T):
                    v.bn_stats(stats[:, t, :], src[t])
                v.drain()
                for t in range(T):
                    last = v.bn_aggr(mv[:, t, :], stats[:, t, :])
                link(last)
                v.tensor_scalar(ve[:, :], mv[:, :, 1], eps, None, ALU.add).then_inc(var_ready.sem, 1)
                v.wait_ge(rstd_ready.sem, rstd_ready.at(layer, i, k))
                for t in range(T):
                    last = v.tensor_scalar(dst[:, t, :], src[t], mv[:, t, 0:1], rstd[:, t:t + 1], ALU.subtract, ALU.mult)
                if gain is not None:
                    link(last)
                    link(v.tensor_tensor(dst[:, :, :], dst[:, :, :], row(gain), ALU.mult))
                    last = v.tensor_tensor(dst[:, :, :], dst[:, :, :], row(add), ALU.add)
                if signal_ is None:
                    link(last)
                else:
                    last.then_inc(signal_.sem, 1)
                    v.wait_ge(signal_.sem, signal_.at(layer, i, state["rows_in"] + 1))
                    state["rows_in"] += 1

            def split(layer, i, n, which):
                for proj, buf, full, parts, bias, lo, done in ((q_proj, score[0], qf, qs, bq, 32, q_split),
                                                              (k_proj, score[1], kf, ks, bk, 64, k_split)):
                    v.wait_ge(proj.sem, proj.at(layer, i, n + 1))
                    src = buf[:, :].rearrange("p (g l) -> p g l", g=G)
                    if which < 2:
                        link(v.tensor_tensor(full[:, :, :], src, bias[:, which, :].unsqueeze(2).broadcast_to((P, G, L)), ALU.add))
                    else:
                        link(v.tensor_copy(full[:, :, :], src))
                    link(v.tensor_copy(parts[:, :, :], full[:, :, :]))
                    v.tensor_tensor(parts[lo:lo + 32, :, :], full[lo:lo + 32, :, :], parts[lo:lo + 32, :, :].bitcast(f32),
                                    ALU.subtract).then_inc(done.sem, 1)
                v.wait_ge(v_proj.sem, v_proj.at(layer, i, n + 1))
                for t in range(T):
                    dst = vp[:, t, :, 0:HD]
                    src = p7[:, t * D:(t + 1) * D].rearrange("p (h d) -> p h d", d=HD)
                    if which < 2:
                        bv = rows[:, ROWS.index(f"{ATTN[which]}_bv"), :].rearrange("p (h d) -> p h d", d=HD)
                        last = v.tensor_tensor(dst, src, bv, ALU.add)
                    else:
                        last = v.tensor_copy(dst, src)
                last.then_inc(v_ready.sem, 1)

            def attend(layer, i, n):
                def divide(u):
                    g, half_ = divmod(u, T)
                    v.wait_ge(pv_turned.sem, pv_turned.at(layer, i, n * UNITS + u + 1))
                    src = p7[:, 0:P].rearrange("p (h c) -> p h c", h=GH)
                    link(v.reciprocal(rden[:, :], src[:, :, HD]))
                    dst = ao[:, half_, g * 32:(g + 1) * 32].rearrange("p (h d) -> p h d", d=HD)
                    v.tensor_tensor(dst, src[:, :, 0:HD], rden[:, :].unsqueeze(2).broadcast_to((P, GH, HD)),
                                    ALU.mult).then_inc(divided.sem, 1)

                for u in range(UNITS):
                    k = n * UNITS + u + 1
                    v.wait_ge(scores_ready.sem, scores_ready.at(layer, i, k))
                    link(v.tensor_reduce(pm[:, :], score[u % 2][:, :].rearrange("p (b c) -> p b c", c=32), AX.X, ALU.max,
                                         apply_transpose=True))
                    v.tensor_tensor(pm2[:, :], pm[:, 0:16], pm[:, 16:32], ALU.max).then_inc(part_max.sem, 1)
                    v.wait_ge(max_turned.sem, max_turned.at(layer, i, k))
                    v.tensor_reduce(nm[:, :], p5[0:16, 0:P].rearrange("p (q m) -> p m q", q=4), AX.X, ALU.max,
                                    negate=True).then_inc(nm_ready.sem, 1)
                    if u:
                        divide(u - 1)
                divide(UNITS - 1)

            def plus(dst, x_, y_, ins_signal=None):
                ins = v.tensor_tensor(dst, x_, y_, ALU.add)
                if ins_signal is None:
                    link(ins)
                else:
                    ins.then_inc(ins_signal.sem, 1)

            def bank7(c=D):
                return p7[:, 0:T * c].rearrange("p (t d) -> p t d", t=T)

            def route(layer, i):
                v.wait_ge(logits_done.sem, logits_done.at(layer, i, 1))
                src = bank7(E)
                link(v.tensor_reduce(red[:, :], src, AX.X, ALU.max))
                v.tensor_tensor(logit[:, :, :], src, red[:, :].unsqueeze(2).broadcast_to((P, T, E)),
                                ALU.subtract).then_inc(centred.sem, 1)
                v.wait_ge(exps_done.sem, exps_done.at(layer, i, 1))
                link(v.tensor_reduce(red[:, :], prob[:, :, :], AX.X, ALU.add))
                link(v.reciprocal(red2[:, :], red[:, :]))
                link(v.tensor_tensor(prob[:, :, :], prob[:, :, :], red2[:, :].unsqueeze(2).broadcast_to((P, T, E)), ALU.mult))
                for t in range(T):
                    other = prob[:, t, :].unsqueeze(1).broadcast_to((P, E, E))
                    own = prob[:, t, :].unsqueeze(2).broadcast_to((P, E, E))
                    v.tensor_tensor(cmp[:, t, :, :], other, own, ALU.is_gt)
                    last = v.tensor_tensor(cmp2[:, t, :, :], other, own, ALU.is_equal)
                link(last)
                lower = const[:, LOWER:LOWER + E * E].unsqueeze(1).broadcast_to((P, T, E * E))
                flat, flat2 = (c[:, :, :, :].rearrange("p t e j -> p t (e j)") for c in (cmp, cmp2))
                link(v.tensor_tensor(flat2, flat2, lower, ALU.mult))
                plus(flat, flat, flat2)
                link(v.tensor_reduce(sel[:, :, :], cmp[:, :, :, :], AX.X, ALU.add))
                link(v.tensor_scalar(sel[:, :, :], sel[:, :, :], 1.5, None, ALU.is_lt))
                if layer == 0:
                    v.tensor_tensor(gate[:, :, :], prob[:, :, :], sel[:, :, :], ALU.mult).then_inc(gates_ready.sem, 1)
                else:
                    link(v.tensor_reduce(red[:, :], prob[:, :, :], AX.X, ALU.max))
                    v.tensor_tensor(logit[:, :, :], prob[:, :, :], red[:, :].unsqueeze(2).broadcast_to((P, T, E)),
                                    ALU.subtract).then_inc(centred.sem, 1)
                    v.wait_ge(exps_done.sem, exps_done.at(layer, i, 2))
                    link(v.tensor_tensor(gate[:, :, :], gate[:, :, :], sel[:, :, :], ALU.mult))
                    link(v.tensor_reduce(red[:, :], gate[:, :, :], AX.X, ALU.add))
                    link(v.reciprocal(red2[:, :], red[:, :]))
                    v.tensor_tensor(gate[:, :, :], gate[:, :, :], red2[:, :].unsqueeze(2).broadcast_to((P, T, E)),
                                    ALU.mult).then_inc(gates_ready.sem, 1)

            def experts(layer, i, acc):
                v.wait_ge(b2_done.sem, b2_done.at(layer, i, 1))
                v.tensor_tensor(acc[:, :, :], acc[:, :, :], bank7(), ALU.add).then_inc(b2_added.sem, 1)
                v.wait_ge(b2_added.sem, b2_added.at(layer, i, 1))
                for e in range(E):
                    v.wait_ge(down_done.sem, down_done.at(layer, i, e + 1))
                    for t in range(T):
                        last = v.scalar_tensor_tensor(acc[:, t, :], p7[:, t * D:(t + 1) * D], gate[:, t, e:e + 1], acc[:, t, :],
                                                      ALU.mult, ALU.add)
                    last.then_inc(acc_done.sem, 1)
                    v.wait_ge(acc_done.sem, acc_done.at(layer, i, e + 1))

            def batch0(i):
                state["n"] = state["rows_in"] = 0
                xb = X[:, bass.ds(i * T, T), :]
                xt = [X[:, bass.ds(i * T + t, 1), :].rearrange("p t d -> p (t d)") for t in range(T)]
                norm(0, i, 1, xt, xn, 1e-5, signal_=rows_in)
                split(0, i, 0, 0)
                for j in range(HEADS // 2):
                    v.wait_ge(qx_proj.sem, qx_proj.at(0, i, j + 1))
                    for h in (2 * j, 2 * j + 1):
                        last = v.scalar_tensor_tensor(qx[:, h, :], (p4, p5)[j % 2][:, (h % 2) * L:(h % 2 + 1) * L],
                                                      bqx[:, h:h + 1], rmask, ALU.add, ALU.mult)
                    last.then_inc(qx_out.sem, 1)
                attend(0, i, 0)
                v.wait_ge(o_proj.sem, o_proj.at(0, i, 1))
                link(v.tensor_tensor(res[:, :, :], bank7(), row("L0_attn_bo"), ALU.add))
                plus(res[:, :, :], res[:, :, :], xb, o_added)
                norm(0, i, 2, [xn[:, t, :] for t in range(T)], n1, 1e-5, "L0_ffn_g1", "L0_ffn_be1", rows_in)
                link(v.tensor_tensor(x1[:, :, :], xn[:, :, :], n1[:, :, :], ALU.add))
                plus(x1[:, :, :], x1[:, :, :], row("L0_ffn_mix_b"))
                v.wait_ge(mix_done.sem, mix_done.at(0, i, 1))
                plus(x1[:, :, :], x1[:, :, :], bank7())
                plus(res[:, :, :], res[:, :, :], x1[:, :, :])
                norm(0, i, 3, [x1[:, t, :] for t in range(T)], n1, 1e-5, "L0_ffn_g2", "L0_ffn_be2", rows_in)
                route(0, i)
                experts(0, i, res)
                link(v.tensor_scalar(xb, res[:, :, :], 1.0, None, ALU.mult))

            def batch1(i):
                state["n"] = state["rows_in"] = 0
                xb = X[:, bass.ds(i * T, T), :]
                xt = [X[:, bass.ds(i * T + t, 1), :].rearrange("p t d -> p (t d)") for t in range(T)]
                norm(1, i, 1, xt, xn, 1e-5, signal_=rows_in)
                split(1, i, 0, 2)
                attend(1, i, 0)
                v.wait_ge(o_proj.sem, o_proj.at(1, i, 1))
                link(v.tensor_tensor(x1[:, :, :], bank7(), row("L1_ffn_bo"), ALU.add))
                plus(x1[:, :, :], x1[:, :, :], xn[:, :, :], o_added)
                v.wait_ge(o_added.sem, o_added.at(1, i, 1))
                norm(1, i, 2, [x1[:, t, :] for t in range(T)], n1, 1e-6, "L1_ffn_ln1_g", "L1_ffn_ln1_b")
                split(1, i, 1, 1)
                attend(1, i, 1)
                v.wait_ge(o_proj.sem, o_proj.at(1, i, 2))
                link(v.tensor_tensor(res[:, :, :], bank7(), row("L1_attn_bo"), ALU.add))
                plus(res[:, :, :], res[:, :, :], xb, o_added)
                v.tensor_copy(x1[:, :, :], n1[:, :, :]).then_inc(rows_in.sem, 1)
                v.wait_ge(rows_in.sem, rows_in.at(1, i, 2))
                route(1, i)
                experts(1, i, x1)
                norm(1, i, 3, [x1[:, t, :] for t in range(T)], n1, 1e-6, "L1_ffn_ln2_g", "L1_ffn_ln2_b")
                v.tensor_tensor(xb, res[:, :, :], n1[:, :, :], ALU.add).then_inc(out_ready.sem, 1)
                v.wait_ge(out_ready.sem, out_ready.at(1, i, 1))

            C0, C1 = CHAIN
            with v.Fori(0, B) as i:
                state["base"] = i * C0 + 1
                batch0(i)
            assert state["n"] == C0, state["n"]
            with v.Fori(0, B) as i:
                state["base"] = i * C1 + (1 + B * C0)
                batch1(i)
            assert state["n"] == C1, state["n"]


CHAIN = (42, 64)

WEIGHTS_T = ["Wq", "Wk", "Wv", "Wo"]


def constants():
    import numpy as np
    c = np.zeros((P, NCONST), np.float32)
    p = np.arange(P)[:, None]
    c[:, EYE:EYE + P] = np.eye(P)
    c[:, RMASK:RMASK + L] = (np.arange(L)[None, :] % RHO) == p // HD
    c[:, HMASK:HMASK + GH] = (p % 32) // HD == np.arange(GH)[None, :]
    c[:16, EYE16:EYE16 + 16] = np.eye(16)
    c[:, LOWER:] = (np.arange(E)[None, :] < np.arange(E)[:, None]).reshape(-1)
    return c


def kernel(**inputs):
    import numpy as np
    import concourse.bacc as bacc
    from concourse.bass_utils import run_bass_kernel_spmd

    nc = bacc.Bacc("TRN2", target_bir_lowering=False, num_devices=1)
    arrays = {"const": constants(), "rows": np.stack([np.asarray(inputs[n]) for n in ROWS])}
    for name, value in inputs.items():
        value = np.asarray(value)
        if name in ROWS:
            continue
        if name[:7] in ("L0_attn", "L1_attn") and name[8:] in WEIGHTS_T or name == "L0_attn_dist_emb":
            value = value.T
        if name[8:] in ("bq", "bk"):
            if name == "L0_attn_bq":
                arrays["bq_heads"] = np.ascontiguousarray(value.reshape(HEADS, HD).T)
            value = value.reshape(G, D // G).T
        if name in ("L0_ffn_b1", "L1_ffn_be1"):
            value = value.reshape(E * FT, P).T
        arrays[name] = np.ascontiguousarray(value)
    a = {n: nc.dram_tensor(f"in_{n}", v.shape, mybir.dt.from_np(v.dtype), kind="ExternalInput").ap() for n, v in arrays.items()}
    out = nc.dram_tensor("out_0", (B, L, D), mybir.dt.float32, kind="ExternalOutput").ap()
    build(nc, a, out)
    r = run_bass_kernel_spmd(nc, [{f"in_{n}": v for n, v in arrays.items()}], core_ids=[0])
    return r.results[0]["out_0"]
```

```python
from contextlib import ExitStack

import concourse.bass as bass
from concourse import mybir

B, L, D = 16, 256, 128
P = 128
T = L // P
HEADS, HD = 16, 8
LEFT, RIGHT = 64, 8
NPOS = LEFT + RIGHT + 1
E, F = 8, 512
FT = F // P
G, GH = 4, 4
UNITS = G * T
RHO = P // HD
ROWS = ["L0_attn_bv", "L0_attn_bo", "L0_ffn_g1", "L0_ffn_be1", "L0_ffn_mix_b", "L0_ffn_g2", "L0_ffn_be2",
        "L1_attn_bv", "L1_attn_bo", "L1_ffn_bo", "L1_ffn_ln1_g", "L1_ffn_ln1_b", "L1_ffn_ln2_g", "L1_ffn_ln2_b"]
ATTN = ["L0_attn", "L1_attn", "L1_ffn"]
EYE, RMASK, HMASK, EYE16, LOWER = 0, 128, 384, 388, 404
SPREAD = LOWER + E * E
NCONST = SPREAD + GH * P


class Batch:

    def __init__(self, c, j=None):
        self.c, self.j = c, j
        self.first = j is None and c == 0

    def __add__(self, n):
        return Batch(self.c + n, self.j)

    def times(self, n, k=0):
        fixed = self.c * n + k
        return fixed if self.j is None else self.j * (2 * n) + fixed


class Signal:

    def __init__(self, sem, layer0, layer1):
        self.sem, self.counts = sem, (layer0, layer1)

    def at(self, layer, i, k):
        return i.times(self.counts[layer], k + layer * B * self.counts[0])


class Tally:

    def __init__(self, per_loop):
        self.base, self.n, self.per_loop = 0, 0, per_loop

    def next(self):
        self.n += 1
        return self.base + self.n

    def enter(self, j):
        self.start = self.base + self.n
        self.base, self.n = j * self.per_loop[0] + self.start, 0

    def leave(self, loops, name):
        per = self.per_loop.pop(0)
        assert self.n == per, f"{name} {self.n} for {per}"
        self.base, self.n = self.start + loops * per, 0


FAR_LEFT = -(-(L // T + LEFT - 1) // RHO) * RHO
FAR_RIGHT = (P - RIGHT + 1) // RHO * RHO
ROOTS = ([(0, 1, 0), (0, 1, 1), (0, 0, 0), (0, 0, 0)], [(0, 0, 0), (0, 0, 1), (0, 1, 0), (1, 0, 0)])

LOOPS = B // 2 - 1


def build(nc, a, out):
    f32, f32r = mybir.dt.float32, mybir.dt.float32r
    ALU, ACT, AX = mybir.AluOpType, mybir.ActivationFunctionType, mybir.AxisListType
    SCALE = float(HD) ** -0.5
    ctx = ExitStack()
    with ctx:
        def sb(name, shape, dt=f32):
            return ctx.enter_context(nc.sbuf_tensor(name, shape, dt))

        def signal(name, layer0=0, layer1=0):
            return Signal(ctx.enter_context(nc.semaphore(name)), layer0, layer1)

        X = sb("X", [P, B * T, D])
        const = sb("const", [P, NCONST])
        rows = sb("rows", [P, len(ROWS), D])
        eye = const[:, EYE:EYE + P]
        rmask = const[:, RMASK:RMASK + L]
        spread = sb("spread", [P, GH, P], f32r)
        wq = sb("wq", [P, 3, G, P])
        wk = sb("wk", [P, 3, G, P])
        wv = sb("wv", [P, 3, D])
        wo = sb("wo", [P, 3, D])
        bq = sb("bq", [P, 2, G])
        bk = sb("bk", [P, 2, G])
        mixw = sb("mixw", [P, D])
        rw = sb("rw", [P, 2, E])
        w1 = sb("w1", [P, E, F])
        w2 = sb("w2", [P, E, FT, D])
        b1 = sb("b1", [P, 2, E, FT])
        b2 = sb("b2", [E, 2, D])
        ext = sb("ext", [HD, 512])
        toep = sb("toep", [P, 496])
        ones16 = sb("ones16", [RHO, P], f32r)
        half = sb("half", [P, T])

        xn = sb("xn", [P, T, D])
        stats = sb("stats", [P, T, 6])
        mv = sb("mv", [P, T, 2])
        ve = sb("ve", [P, T])
        rstd = sb("rstd", [P, T])
        xT = sb("xT", [P, L])
        n1T = sb("n1T", [P, L])
        hidT = sb("hidT", [P, 2, L])
        full = sb("full", [P, G, L])
        qs = sb("qs", [P, 2, G, L], f32r)
        ks = sb("ks", [P, 2, G, L], f32r)
        qm = sb("qm", [P, 2, GH, L], f32r)
        qx = sb("qx", [P, 2, GH, L])
        vp = sb("vp", [P, 2, T, HEADS, 32])
        pm = sb("pm", [P, 32])
        pm2 = sb("pm2", [P, 2, 16])
        nm = sb("nm", [16, 2, 32])
        ksa = sb("ksa", [P, 2, G, L], f32r)
        far = sb("far", [P, T])
        shift = sb("shift", [16, 2, 16, 32], f32r)
        probs = sb("probs", [P, 2, T, GH * P])
        pv = sb("pv", [P, P])
        rden = sb("rden", [P, GH])
        ao = sb("ao", [P, 2, T, D])
        aoT = sb("aoT", [P, L])
        n1 = sb("n1", [P, T, D])
        x1 = sb("x1", [P, T, D])
        acc = sb("acc", [P, 2, T, D])
        res = sb("res", [P, 2, T, D])
        hT = sb("hT", [P, 2, FT, L])
        logit = sb("logit", [P, T, E])
        prob = sb("prob", [P, T, E])
        eprob = sb("eprob", [P, T, E])
        red = sb("red", [P, T])
        red2 = sb("red2", [P, T])
        cmp = sb("cmp", [P, T, E, E])
        cmp2 = sb("cmp2", [P, T, E, E])
        sel = sb("sel", [P, T, E])
        gate = sb("gate", [P, 2, T, E])
        gT = sb("gT", [E, L])

        score = [ctx.enter_context(nc.psum_tensor(f"score{n}", [P, 1024], f32)) for n in range(2)]
        p4, p5, p6, p7 = [ctx.enter_context(nc.psum_tensor(f"bank{n}", [P, 512], f32)) for n in range(4, 8)]

        loaded, weights0, weights1, shifts_loaded, stored, ext_ready, ready = (
            ctx.enter_context(nc.semaphore(n)) for n in
            ("loaded", "weights0", "weights1", "shifts_loaded", "stored", "ext_ready", "ready"))
        dve = signal("dve")
        bank7_read = signal("bank7_read")
        var_ready = signal("var_ready")
        rstd_ready = signal("rstd_ready")
        xn_ready = signal("xn_ready", 1, 1)
        n1_ready = signal("n1_ready", 1, 0)
        hid_ready = signal("hid_ready", 1, 1)
        xn_turned = signal("xn_turned", 1, 1)
        n1_turned = signal("n1_turned", 1, 0)
        hid_turned = signal("hid_turned", 1, 1)
        ao_turned = signal("ao_turned", 1, 2)
        xT_out = signal("xT_out", 1, 1)
        n1T_out = signal("n1T_out", 1, 0)
        hidT_out = signal("hidT_out", 1, 1)
        aoT_out = signal("aoT_out", 1, 2)
        q_proj = signal("q_proj", 2, 4)
        k_proj = signal("k_proj", 2, 4)
        v_proj = signal("v_proj", 1, 2)
        q_split = signal("q_split", 1, 2)
        k_split = signal("k_split", 1, 2)
        v_ready = signal("v_ready", 1, 2)
        q_masked = signal("q_masked", G, 2 * G)
        qx_proj = signal("qx_proj", 2 * G, 0)
        qx_out = signal("qx_out", 2 * G, 0)
        scores_ready = signal("scores_ready", UNITS, 2 * UNITS)
        part_max = signal("part_max", UNITS, 2 * UNITS)
        max_turned = signal("max_turned", UNITS, 2 * UNITS)
        nm_ready = signal("nm_ready", UNITS, 2 * UNITS)
        shift_rows = signal("shift_rows", UNITS, 2 * UNITS)
        shifted = signal("shifted", UNITS, 2 * UNITS)
        probs_ready = signal("probs_ready", UNITS, 2 * UNITS)
        pv_done = signal("pv_done", UNITS, 2 * UNITS)
        pv_out = signal("pv_out", UNITS, 2 * UNITS)
        pv_turned = signal("pv_turned", UNITS, 2 * UNITS)
        divided = signal("divided", UNITS, 2 * UNITS)
        o_proj = signal("o_proj", 1, 2)
        mix_done = signal("mix_done", 1, 0)
        logits_done = signal("logits_done", 1, 1)
        centred = signal("centred", 1, 2)
        exps_done = signal("exps_done", 1, 2)
        gates_ready = signal("gates_ready", 1, 1)
        gates_turned = signal("gates_turned", 1, 1)
        gates_out = signal("gates_out", 1, 1)
        b2_done = signal("b2_done", 1, 1)
        up_done = signal("up_done", 2 * E, 2 * E)
        act_done = signal("act_done", 2 * E, 2 * E)
        down_done = signal("down_done", E, E)
        out_ready = signal("out_ready", 0, 1)

        def row(name):
            return rows[:, ROWS.index(name), :].unsqueeze(1).broadcast_to((P, T, D))

        def attention(layer, i_par, n):
            return (0, i_par) if layer == 0 else ((2, 0), (1, 1))[n]

        def pairs_of(layer, s):
            return [(0, s)] if layer == 0 else [(s // 2, 2 * (s % 2)), (s // 2, 2 * (s % 2) + 1)]

        def following(layer, n, g):
            if g + 1 < G:
                return 0, n, g + 1
            return (0, 1, 0) if layer == 1 and n == 0 else (1, 0, 0)

        def run(eng, tallies, iteration):
            for layer in range(2):
                iteration(layer, Batch(-2), 0, False, False, True)
                iteration(layer, Batch(-1), 1, False, True, True)
                with eng.Fori(0, LOOPS) as j:
                    for t in tallies:
                        t.enter(j)
                    iteration(layer, Batch(0, j), 0, True, True, True)
                    iteration(layer, Batch(1, j), 1, True, True, True)
                for name, t in zip("abc", tallies):
                    t.leave(LOOPS, f"layer {layer} {name}")
                iteration(layer, Batch(B - 2), 0, True, True, False)
                iteration(layer, Batch(B - 1), 1, True, False, False)

        counts = {}
        block = ctx.enter_context(nc.Block())

        @block.sync
        def _(sp):
            def load(sem, dst, src):
                sp.dma_start(dst, src).then_inc(sem, 16)
                counts[sem] = counts.get(sem, 0) + 16

            def experts(layer, sem):
                names = (("w1", "w2"), ("We1", "We2"))[layer]
                load(sem, w1[:, :, :], a[f"L{layer}_ffn_{names[0]}"].rearrange("e p f -> p e f"))
                load(sem, w2[:, :, :, :].rearrange("p e t d -> p (e t) d"),
                     a[f"L{layer}_ffn_{names[1]}"].rearrange("e (t p) d -> p (e t) d", p=P))

            x = a["L0_attn_hidden_states"].rearrange("b (t p) d -> p (b t) d", p=P)
            for r in range(P // HD):
                load(loaded, far[HD * r:HD * r + HD, :], a["far"])
            sp.dma_start(ext[:, 192:192 + NPOS], a["L0_attn_dist_emb"]).then_inc(shifts_loaded, 16)
            load(loaded, const[:, :], a["const"])
            load(loaded, X[:, :, :], x)
            load(loaded, rows[:, :, :], a["rows"].partition_broadcast(P))
            for n, name in enumerate(ATTN):
                for w, key in ((wq, "Wq"), (wk, "Wk")):
                    src = a[f"{name}_{key}"].rearrange("p (g c) -> p g c", g=G)
                    for copy in range(4):
                        load(loaded, w[:, n, :, 32 * copy:32 * copy + 32], src)
                load(loaded, wv[:, n, :], a[f"{name}_Wv"])
                load(loaded, wo[:, n, :], a[f"{name}_Wo"])
                if n < 2:
                    for b, key in ((bq, "bq"), (bk, "bk")):
                        for copy in range(4):
                            load(loaded, b[32 * copy:32 * copy + 32, n, :], a[f"{name}_{key}"])
            load(loaded, mixw[:, :], a["L0_ffn_mix_w"])
            for n, (r, bu, bd) in enumerate((("router_w", "b1", "b2"), ("Wr", "be1", "be2"))):
                load(loaded, rw[:, n, :], a[f"L{n}_ffn_{r}"])
                load(loaded, b1[:, n, :, :].rearrange("p e t -> p (e t)"), a[f"L{n}_ffn_{bu}"])
                load(loaded, b2[:, n, :], a[f"L{n}_ffn_{bd}"])
            sp.wait_ge(ext_ready, 2)
            for r in range(RHO):
                sp.dma_start(toep[HD * r:HD * r + HD, :], ext[:, 16 - r:16 - r + 496]).then_inc(shifts_loaded, 16)
            experts(0, weights0)
            sp.wait_ge(down_done.sem, down_done.at(0, Batch(B - 1), E))
            experts(1, weights1)
            y = out.rearrange("b (t p) d -> b p t d", p=P)
            with sp.Fori(0, B) as i:
                sp.wait_ge(out_ready.sem, i + 1)
                sp.dma_start(y[bass.ds(i, 1)].rearrange("b p t d -> p (b t) d"), X[:, bass.ds(i * T, T), :]).then_inc(stored, 16)
            sp.wait_ge(stored, 16 * B)

        @block.gpsimd
        def _(pool):
            pool.memset(half[:, :], -0.5).then_inc(ready, 1)
            pool.memset(ones16[:, :].bitcast(f32), 1.0).then_inc(ready, 1)
            pool.memset(vp[:, :, :, :, :], 0.0).then_inc(ready, 1)
            pool.wait_ge(ready, 3)
            pool.memset(vp[:, :, :, :, HD:HD + 1], 1.0).then_inc(ready, 1)
            pool.wait_ge(loaded, counts[loaded])
            pool.tensor_copy(spread[:, :, :], const[:, SPREAD:].rearrange("p (h c) -> p h c", h=GH)).then_inc(ready, 1)
            pool.wait_ge(ready, 5)
            roots = Tally(LOOP_ROOTS[:])

            def root():
                pool.wait_ge(var_ready.sem, roots.next())
                pool.tensor_tensor(rstd[:, :], ve[:, :], half[:, :], ALU.pow).then_inc(rstd_ready.sem, 1)

            def mask(layer, i, par, n, g):
                _, set_ = attention(layer, par, n)
                if g == 0:
                    pool.wait_ge(q_split.sem, q_split.at(layer, i, n + 1))
                if not (i.first and n == 0 and g < 2 and layer == 0):
                    pool.wait_ge(scores_ready.sem, scores_ready.at(layer, i, T * (n * G + g - 1)))
                pool.tensor_tensor(qm[0:96, g % 2, :, :],
                                   qs[0:96, set_, g, :].bitcast(f32).unsqueeze(1).broadcast_to((96, GH, L)),
                                   const[0:96, HMASK:HMASK + GH].unsqueeze(2).broadcast_to((96, GH, L)),
                                   ALU.mult).then_inc(q_masked.sem, 1)

            def iteration(layer, it, par, F_, A_, N_):
                for s in range(G):
                    if A_:
                        for n, g in pairs_of(layer, s):
                            on, n2, g2 = following(layer, n, g)
                            if not on:
                                mask(layer, it + 1, 1 - par, n2, g2)
                    for _ in range(sum(r * there for r, there in zip(ROOTS[layer][s], (F_, A_, N_)))):
                        root()
                if N_:
                    mask(layer, it + 2, par, 0, 0)

            run(pool, [roots], iteration)

        @block.scalar
        def _(act):
            act.wait_ge(loaded, counts[loaded])

            def take(turned, out_, layer, i, k, dst, rows_=P):
                act.wait_ge(turned.sem, turned.at(layer, i, k))
                act.activation(dst, p7[0:rows_, 0:L], ACT.Copy).then_inc(out_.sem, 1)
                act.wait_ge(out_.sem, out_.at(layer, i, k))
                act.sem_inc(bank7_read.sem, 1)

            def hidden(layer, i, e, pair):
                act.wait_ge(up_done.sem, up_done.at(layer, i, 2 * e + pair + 1))
                for ft in (2 * pair, 2 * pair + 1):
                    last = act.activation(hT[:, e % 2, ft, :], (p4, p5)[pair][:, (ft % 2) * L:(ft % 2 + 1) * L],
                                          (ACT.Silu, ACT.Gelu)[layer], bias=b1[:, layer, e, ft:ft + 1])
                last.then_inc(act_done.sem, 1)

            def exp(layer, i, n, u):
                act.wait_ge(shifted.sem, shifted.at(layer, i, n * UNITS + u + 1))
                act.activation(probs[:, u % 2, :, :].rearrange("p t c -> p (t c)"), score[u % 2][:, :], ACT.Exp,
                               scale=SCALE).then_inc(probs_ready.sem, 1)

            def take_values(layer, i, k):
                act.wait_ge(pv_done.sem, pv_done.at(layer, i, k))
                act.activation(pv[:, :], p6[:, 0:P], ACT.Copy).then_inc(pv_out.sem, 1)

            def centre_exp(layer, i, k, src, dst):
                act.wait_ge(centred.sem, centred.at(layer, i, k))
                act.activation(dst[:, :, :], src[:, :, :], ACT.Exp).then_inc(exps_done.sem, 1)

            def extra(layer, s, x, f, b, nx, par, F_, A_, N_):
                at = (layer, s, x)
                if F_ and at == (0, 0, 3):
                    take(ao_turned, aoT_out, 0, f, 1, aoT[:, :])
                if F_ and at == (1, 0, 2):
                    take(ao_turned, aoT_out, 1, f, 2, aoT[:, :])
                if A_ and at == (0, 1, 2):
                    take(n1_turned, n1T_out, 0, b, 1, n1T[:, :])
                if A_ and at == (0, 2, 2) or A_ and at == (1, 2, 5):
                    take(hid_turned, hidT_out, layer, b, 1, hidT[:, 1 - par, :])
                if A_ and at == (1, 2, 2):
                    take(ao_turned, aoT_out, 1, b, 1, aoT[:, :])
                if A_ and at == (0, 2, 6):
                    centre_exp(0, b, 1, logit, prob)
                if A_ and at == (1, 2, 6):
                    centre_exp(1, b, 1, logit, prob)
                    centre_exp(1, b, 2, logit, eprob)
                if A_ and at in ((0, 3, 3), (1, 3, 2)):
                    take(gates_turned, gates_out, layer, b, 1, gT[:, :], E)
                if N_ and at in ((0, 2, 4), (1, 2, 0)):
                    take(xn_turned, xT_out, layer, nx, 1, xT[:, :])

            def iteration(layer, it, par, F_, A_, N_):
                f, b, nx = it, it + 1, it + 2
                for s in range(G):
                    def more(x):
                        extra(layer, s, x, f, b, nx, par, F_, A_, N_)
                    n, g = pairs_of(layer, s)[0]
                    k = T * (n * G + g)
                    tail = A_ if s else F_
                    if F_:
                        hidden(layer, f, 2 * s, 0)
                    more(0)
                    if F_:
                        hidden(layer, f, 2 * s, 1)
                    if tail:
                        take_values(layer, b, k - 1)
                    if layer == 0:
                        more(1)
                    if F_:
                        hidden(layer, f, 2 * s + 1, 0)
                    if tail:
                        take_values(layer, b, k)
                    if layer == 1:
                        more(1)
                    else:
                        more(2)
                    if F_:
                        hidden(layer, f, 2 * s + 1, 1)
                    if layer == 0:
                        more(3)
                    if A_:
                        exp(layer, b, n, T * g)
                    more(4 if layer == 0 else 2)
                    if A_:
                        exp(layer, b, n, T * g + 1)
                    if layer == 0:
                        more(5)
                        more(6)
                        continue
                    more(3)
                    n, g = pairs_of(layer, s)[1]
                    if A_:
                        take_values(layer, b, k + 1)
                        take_values(layer, b, k + 2)
                    more(4)
                    if A_:
                        exp(layer, b, n, T * g)
                    more(5)
                    if A_:
                        exp(layer, b, n, T * g + 1)
                    more(6)

            run(act, [], iteration)

        @block.tensor
        def _(pe):
            pe.wait_ge(loaded, counts[loaded])
            pe.wait_ge(ready, 5)
            pe.wait_ge(shifts_loaded, 16 * (1 + RHO))
            bank7 = Tally(LOOP_BANK7[:])
            used = {"once": False}

            def open7():
                value = bank7.next()
                if used["once"]:
                    pe.wait_ge(bank7_read.sem, value - 1)
                used["once"] = True

            def turn(src, turned, rows_=P):
                open7()
                for t in range(T):
                    last = pe.transpose(p7[0:rows_, t * P:(t + 1) * P], src[:, t, :], eye)
                last.then_inc(turned.sem, 1)

            def by_token(lhs, w, done):
                open7()
                c = w.shape[-1]
                for t in range(T):
                    last = pe.matmul(p7[:, t * c:(t + 1) * c], lhs[:, t * P:(t + 1) * P], w, start=True, stop=True)
                last.then_inc(done.sem, 1)

            def project(w, n, pair, done):
                open7()
                for g in (2 * pair, 2 * pair + 1):
                    last = pe.matmul(p7[:, (g % 2) * L:(g % 2 + 1) * L], w[:, n, g, :], xT[:, :], start=True, stop=True)
                last.then_inc(done.sem, 1)

            def spread_queries(layer, i, par, g, pair):
                open7()
                for h in range(2):
                    last = pe.matmul(p7[:, h * L:(h + 1) * L], spread[0:64, 2 * pair + h, :], qs[0:64, par, g, :],
                                     start=True, stop=True)
                last.then_inc(qx_proj.sem, 1)

            def scores(layer, i, par, n, u):
                g, half_ = divmod(u, T)
                _, set_ = attention(layer, par, n)
                k = n * UNITS + u + 1
                if not (i.first and layer == 0 and k <= 2):
                    pe.wait_ge(probs_ready.sem, probs_ready.at(layer, i, k - 2))
                if half_ == 0:
                    pe.wait_ge(q_masked.sem, q_masked.at(layer, i, n * G + g + 1))
                    if g == 0:
                        pe.wait_ge(k_split.sem, k_split.at(layer, i, n + 1))
                        pe.wait_ge(v_ready.sem, v_ready.at(layer, i, n + 1))
                    if layer == 0:
                        pe.wait_ge(qx_out.sem, qx_out.at(layer, i, 2 * g + 2))
                for kb in range(T):
                    dst = score[u % 2][:, kb * 512:(kb + 1) * 512]
                    keys = ks[0:96, set_, g, kb * P:(kb + 1) * P]
                    view = dst.rearrange("p (h l) -> p h l", h=GH)
                    if layer == 1 or kb == half_:
                        last = pe.matmul(dst, keys, qm[0:96, g % 2, :, half_ * P:(half_ + 1) * P], start=True, stop=layer == 1)
                        near = (0, P)
                    else:
                        near = (0, P - (L - FAR_LEFT)) if kb == 0 else (FAR_RIGHT, P)
                        for (lo, hi), stationary, start in ((near, keys, True),
                                                            (((near[1], P) if kb == 0 else (0, near[0])),
                                                             ksa[0:96, set_, g, kb * P:(kb + 1) * P], False)):
                            last = pe.matmul(view[:, :, lo:hi], stationary,
                                             qm[0:96, g % 2, :, half_ * P + lo:half_ * P + hi], start=start, stop=True,
                                             skip_group_check=True)
                    if layer == 0:
                        for m in range(near[0] // RHO, near[1] // RHO):
                            l0 = half_ * P + m * RHO
                            at = kb * P - l0 + 240
                            last = pe.matmul(view[:, :, m * RHO:(m + 1) * RHO], toep[:, at:at + P],
                                             qx[:, g % 2, :, l0:l0 + RHO], start=False, stop=m == near[1] // RHO - 1,
                                             skip_group_check=kb != half_)
                last.then_inc(scores_ready.sem, 1)

            def turn_max(layer, i, n, u):
                k = n * UNITS + u + 1
                pe.wait_ge(part_max.sem, part_max.at(layer, i, k))
                if not (i.first and layer == 0 and k <= 2):
                    pe.wait_ge(divided.sem, divided.at(layer, i, k - 2))
                pe.transpose(p6[0:16, 256:256 + P], pm2[:, u % 2, :], eye).then_inc(max_turned.sem, 1)

            def subtract(layer, i, n, u):
                pe.wait_ge(shift_rows.sem, shift_rows.at(layer, i, n * UNITS + u + 1))
                for kb in range(T):
                    last = pe.matmul(score[u % 2][:, kb * 512:(kb + 1) * 512], ones16[:, :],
                                     shift[:, u % 2, :, :].rearrange("p a b -> p (a b)"), start=False, stop=True,
                                     skip_group_check=True)
                last.then_inc(shifted.sem, 1)

            def values(layer, i, par, n, u, last_batch):
                _, set_ = attention(layer, par, n)
                g = u // T
                k = n * UNITS + u + 1
                pe.wait_ge(probs_ready.sem, probs_ready.at(layer, i, k))
                if last_batch and k == (1 + layer) * UNITS:
                    pe.wait_ge(divided.sem, divided.at(layer, i, k - 1))
                else:
                    pe.wait_ge(nm_ready.sem, nm_ready.at(layer, i, k + 1))
                for kb in range(T):
                    for h in range(GH):
                        last = pe.matmul(p6[32 * h:32 * h + 32, 0:P], vp[:, set_, kb, g * GH + h, :],
                                         probs[:, u % 2, kb, h * P:(h + 1) * P], start=kb == 0, stop=kb == T - 1)
                last.then_inc(pv_done.sem, 1)

            def turn_values(layer, i, par, n, u):
                pe.wait_ge(pv_out.sem, pv_out.at(layer, i, n * UNITS + u + 1))
                pe.transpose(p6[:, P:2 * P], pv[:, :], eye).then_inc(pv_turned.sem, 1)

            def extra(layer, s, x, f, b, nx, par, F_, A_, N_):
                at = (layer, s, x)
                odd = 1 - par

                def take_in(ready_, i, k, src, turned, rows_=P):
                    pe.wait_ge(ready_.sem, ready_.at(layer, i, k))
                    turn(src, turned, rows_)

                def product(out_, i, k, lhs, w, done):
                    pe.wait_ge(out_.sem, out_.at(layer, i, k))
                    by_token(lhs, w, done)

                if layer == 0:
                    if A_ and s < G - 1 and x < 2:
                        spread_queries(0, b, odd, s + 1, x)
                    if F_ and at == (0, 0, 3):
                        take_in(divided, f, UNITS, ao[:, par], ao_turned)
                    if F_ and at == (0, 0, 4):
                        product(aoT_out, f, 1, aoT, wo[:, 0, :], o_proj)
                    if A_ and at == (0, 1, 2):
                        take_in(n1_ready, b, 1, n1, n1_turned)
                    if A_ and at == (0, 1, 3):
                        product(n1T_out, b, 1, n1T, mixw[:, :], mix_done)
                    if A_ and at == (0, 2, 2):
                        take_in(hid_ready, b, 1, n1, hid_turned)
                    if A_ and at == (0, 2, 3):
                        product(hidT_out, b, 1, hidT[:, odd, :], rw[:, 0, :], logits_done)
                    if N_ and at == (0, 2, 4):
                        take_in(xn_ready, nx, 1, xn, xn_turned)
                    if N_ and at == (0, 2, 5):
                        pe.wait_ge(xT_out.sem, xT_out.at(0, nx, 1))
                        project(wq, 0, 0, q_proj)
                    if N_ and at == (0, 3, 0):
                        project(wq, 0, 1, q_proj)
                    if N_ and s == 3 and x in (1, 2):
                        project(wk, 0, x - 1, k_proj)
                    if A_ and at == (0, 3, 3):
                        take_in(gates_ready, b, 1, gate[:, odd], gates_turned, E)
                    if A_ and at == (0, 3, 4):
                        product(gates_out, b, 1, gT, b2[:, 0, :], b2_done)
                    if N_ and at == (0, 3, 5):
                        by_token(xT, wv[:, 0, :], v_proj)
                    if N_ and at == (0, 3, 6):
                        pe.wait_ge(q_split.sem, q_split.at(0, nx, 1))
                        spread_queries(0, nx, par, 0, 0)
                        spread_queries(0, nx, par, 0, 1)
                    return
                if A_ and s == 0 and x in (0, 1):
                    project(wq, 1, x, q_proj)
                if A_ and s == 0 and x in (4, 5):
                    project(wk, 1, x - 4, k_proj)
                if A_ and at == (1, 0, 6):
                    by_token(xT, wv[:, 1, :], v_proj)
                if F_ and at == (1, 0, 2):
                    take_in(divided, f, 2 * UNITS, ao[:, 1], ao_turned)
                if F_ and at == (1, 0, 3):
                    product(aoT_out, f, 2, aoT, wo[:, 1, :], o_proj)
                if N_ and at == (1, 2, 0):
                    take_in(xn_ready, nx, 1, xn, xn_turned)
                if N_ and s == 2 and x in (1, 4):
                    pe.wait_ge(xT_out.sem, xT_out.at(1, nx, 1))
                    project(wq, 2, x // 4, q_proj)
                if A_ and at == (1, 2, 2):
                    take_in(divided, b, UNITS, ao[:, 0], ao_turned)
                if A_ and at == (1, 2, 3):
                    product(aoT_out, b, 1, aoT, wo[:, 2, :], o_proj)
                if A_ and at == (1, 2, 5):
                    take_in(hid_ready, b, 1, acc[:, odd], hid_turned)
                if A_ and at == (1, 2, 6):
                    product(hidT_out, b, 1, hidT[:, odd, :], rw[:, 1, :], logits_done)
                if N_ and s == 3 and x in (0, 1):
                    project(wk, 2, x, k_proj)
                if A_ and at == (1, 3, 2):
                    take_in(gates_ready, b, 1, gate[:, odd], gates_turned, E)
                if A_ and at == (1, 3, 3):
                    product(gates_out, b, 1, gT, b2[:, 1, :], b2_done)
                if N_ and at == (1, 3, 4):
                    by_token(xT, wv[:, 2, :], v_proj)

            def up(layer, i, par, e, pair):
                if e:
                    pe.wait_ge(act_done.sem, act_done.at(layer, i, 2 * (e - 1) + pair + 1))
                for ft in (2 * pair, 2 * pair + 1):
                    last = pe.matmul((p4, p5)[pair][:, (ft % 2) * L:(ft % 2 + 1) * L],
                                     w1[:, e, ft * P:(ft + 1) * P], hidT[:, par, :], start=True, stop=True)
                last.then_inc(up_done.sem, 1)

            def down(layer, i, e):
                pe.wait_ge(act_done.sem, act_done.at(layer, i, 2 * e + 2))
                open7()
                for t in range(T):
                    for ft in range(FT):
                        last = pe.matmul(p7[:, t * D:(t + 1) * D], hT[:, e % 2, ft, t * P:(t + 1) * P],
                                         w2[:, e, ft, :], start=ft == 0, stop=ft == FT - 1)
                last.then_inc(down_done.sem, 1)

            def iteration(layer, it, par, F_, A_, N_):
                f, b, nx, odd = it, it + 1, it + 2, 1 - par
                if A_ and not F_:
                    pe.wait_ge((weights0, weights1)[layer], counts[(weights0, weights1)[layer]])
                tail = [(f, par, layer, UNITS - 2), (f, par, layer, UNITS - 1)] if F_ else []
                only = F_ and not A_
                for s in range(G):
                    def more(x):
                        extra(layer, s, x, f, b, nx, par, F_, A_, N_)

                    n, g = pairs_of(layer, s)[0]
                    u = T * g
                    if F_:
                        up(layer, f, par, 2 * s, 0)
                    more(0)
                    if A_:
                        scores(layer, b, odd, n, u)
                    if F_:
                        up(layer, f, par, 2 * s, 1)
                    if tail:
                        values(layer, *tail[0], only)
                    if layer == 0:
                        more(1)
                    if A_:
                        scores(layer, b, odd, n, u + 1)
                    if tail:
                        turn_values(layer, *tail[0])
                    if layer == 0 and A_:
                        turn_max(layer, b, n, u)
                    if F_:
                        up(layer, f, par, 2 * s + 1, 0)
                    if layer == 1 and A_:
                        turn_max(layer, b, n, u)
                    if tail:
                        values(layer, *tail[1], only)
                    more(2 if layer == 0 else 1)
                    if tail:
                        turn_values(layer, *tail[1])
                    tail = []
                    if F_:
                        up(layer, f, par, 2 * s + 1, 1)
                    if A_:
                        turn_max(layer, b, n, u + 1)
                    if layer == 0:
                        more(3)
                    if A_:
                        subtract(layer, b, n, u)
                    if layer == 1:
                        more(2)
                    if F_ and layer == 0:
                        down(layer, f, 2 * s)
                        more(4)
                    elif layer == 0:
                        more(4)
                    if A_:
                        subtract(layer, b, n, u + 1)
                        tail = [(b, odd, n, u), (b, odd, n, u + 1)]
                    if layer == 0:
                        if F_:
                            down(layer, f, 2 * s + 1)
                        more(5)
                        more(6)
                        continue
                    n, g = pairs_of(layer, s)[1]
                    u = T * g
                    if F_:
                        down(layer, f, 2 * s)
                    if A_:
                        scores(layer, b, odd, n, u)
                    more(3)
                    if A_:
                        values(layer, *tail[0], False)
                        scores(layer, b, odd, n, u + 1)
                        turn_values(layer, *tail[0])
                    if F_:
                        down(layer, f, 2 * s + 1)
                    if A_:
                        turn_max(layer, b, n, u)
                        values(layer, *tail[1], False)
                    more(4)
                    if A_:
                        turn_values(layer, *tail[1])
                        turn_max(layer, b, n, u + 1)
                        subtract(layer, b, n, u)
                    more(5)
                    if A_:
                        subtract(layer, b, n, u + 1)
                        tail = [(b, odd, n, u), (b, odd, n, u + 1)]
                    more(6)

            run(pe, [bank7], iteration)

        @block.vector
        def _(v):
            v.wait_ge(shifts_loaded, 16)
            v.memset(ext[:, 0:192], 0.0)
            v.memset(ext[:, 192 + NPOS:512], 0.0).then_inc(dve.sem, 1)
            steps = Tally(LOOP_STEPS[:])
            roots = Tally(LOOP_ROOTS[:])
            v.wait_ge(dve.sem, steps.next())
            v.tensor_scalar(ext[:, 0:192], ext[:, 0:192], ext[:, 192:193], None, ALU.add).then_inc(ext_ready, 1)
            v.tensor_scalar(ext[:, 192 + NPOS:512], ext[:, 192 + NPOS:512], ext[:, 191 + NPOS:192 + NPOS], None,
                            ALU.add).then_inc(ext_ready, 1)
            v.wait_ge(loaded, counts[loaded])
            v.wait_ge(ready, 5)
            def link(ins):
                ins.then_inc(dve.sem, 1)
                v.wait_ge(dve.sem, steps.next())

            def close7():
                v.sem_inc(bank7_read.sem, 1)

            def bank7(c=D):
                return p7[:, 0:T * c].rearrange("p (t d) -> p t d", t=T)

            def plus(dst, x_, y_):
                link(v.tensor_tensor(dst, x_, y_, ALU.add))

            def norm(src, dst, eps, gain=None, add=None, done=None):
                for t in range(T):
                    v.bn_stats(stats[:, t, :], src[t])
                v.drain()
                for t in range(T):
                    last = v.bn_aggr(mv[:, t, :], stats[:, t, :])
                link(last)
                v.tensor_scalar(ve[:, :], mv[:, :, 1], eps, None, ALU.add).then_inc(var_ready.sem, 1)
                v.wait_ge(rstd_ready.sem, roots.next())
                for t in range(T):
                    last = v.tensor_scalar(dst[:, t, :], src[t], mv[:, t, 0:1], rstd[:, t:t + 1], ALU.subtract, ALU.mult)
                if gain is not None:
                    link(last)
                    link(v.tensor_tensor(dst[:, :, :], dst[:, :, :], row(gain), ALU.mult))
                    last = v.tensor_tensor(dst[:, :, :], dst[:, :, :], row(add), ALU.add)
                link(last)
                if done is not None:
                    v.sem_inc(done.sem, 1)

            def take_half(layer, i, par, n, pair, dst, bias, proj):
                which, _ = attention(layer, par, n)
                v.wait_ge(proj.sem, proj.at(layer, i, 2 * n + pair + 1))
                src = p7[:, :].rearrange("p (g l) -> p g l", g=2)
                dst = dst[:, 2 * pair:2 * pair + 2, :]
                if which < 2:
                    link(v.tensor_tensor(dst, src, bias[:, which, 2 * pair:2 * pair + 2].unsqueeze(2)
                                         .broadcast_to((P, 2, L)), ALU.add))
                else:
                    link(v.tensor_copy(dst, src))
                close7()

            def split(layer, i, par, n, parts, lo, done):
                _, set_ = attention(layer, par, n)
                link(v.tensor_copy(parts[0:96, set_, :, :], full[0:96, :, :]))
                v.tensor_tensor(parts[lo:lo + 32, set_, :, :], full[lo:lo + 32, :, :],
                                parts[lo:lo + 32, set_, :, :].bitcast(f32), ALU.subtract).then_inc(done.sem, 1)
                v.wait_ge(done.sem, done.at(layer, i, n + 1))

            def far_keys(par):
                for t in range(T):
                    part = full[:, :, t * P:(t + 1) * P]
                    last = v.tensor_scalar(part, part, far[:, t:t + 1], None, ALU.add)
                link(last)
                link(v.tensor_copy(ksa[0:96, par, :, :], full[0:96, :, :]))
                link(v.tensor_tensor(ksa[64:96, par, :, :], full[64:96, :, :], ksa[64:96, par, :, :].bitcast(f32), ALU.subtract))

            def take_v(layer, i, par, n):
                which, set_ = attention(layer, par, n)
                v.wait_ge(v_proj.sem, v_proj.at(layer, i, n + 1))
                for t in range(T):
                    dst = vp[:, set_, t, :, 0:HD]
                    src = p7[:, t * D:(t + 1) * D].rearrange("p (h d) -> p h d", d=HD)
                    if which < 2:
                        bv = rows[:, ROWS.index(f"{ATTN[which]}_bv"), :].rearrange("p (h d) -> p h d", d=HD)
                        last = v.tensor_tensor(dst, src, bv, ALU.add)
                    else:
                        last = v.tensor_copy(dst, src)
                last.then_inc(v_ready.sem, 1)
                v.wait_ge(v_ready.sem, v_ready.at(layer, i, n + 1))
                close7()

            def mask_spread(layer, i, g, pair):
                v.wait_ge(qx_proj.sem, qx_proj.at(layer, i, 2 * g + pair + 1))
                v.tensor_tensor(qx[:, g % 2, 2 * pair:2 * pair + 2, :], p7[:, :].rearrange("p (h l) -> p h l", h=2),
                                rmask.unsqueeze(1).broadcast_to((P, 2, L)), ALU.mult).then_inc(qx_out.sem, 1)
                v.wait_ge(qx_out.sem, qx_out.at(layer, i, 2 * g + pair + 1))
                close7()

            def partial_max(layer, i, n, u):
                v.wait_ge(scores_ready.sem, scores_ready.at(layer, i, n * UNITS + u + 1))
                link(v.tensor_reduce(pm[:, :], score[u % 2][:, :].rearrange("p (b c) -> p b c", c=32), AX.X, ALU.max,
                                     apply_transpose=True))
                v.tensor_tensor(pm2[:, u % 2, :], pm[:, 0:16], pm[:, 16:32], ALU.max).then_inc(part_max.sem, 1)

            def minus_max(layer, i, n, u):
                v.wait_ge(max_turned.sem, max_turned.at(layer, i, n * UNITS + u + 1))
                v.tensor_reduce(nm[:, u % 2, :], p6[0:16, 256:256 + P].rearrange("p (q m) -> p m q", q=4), AX.X, ALU.max,
                                negate=True).then_inc(nm_ready.sem, 1)
                v.wait_ge(nm_ready.sem, nm_ready.at(layer, i, n * UNITS + u + 1))
                v.tensor_tensor(shift[:, u % 2, :, :], nm[:, u % 2, :].unsqueeze(1).broadcast_to((16, 16, 32)),
                                const[0:16, EYE16:EYE16 + 16].unsqueeze(2).broadcast_to((16, 16, 32)),
                                ALU.mult).then_inc(shift_rows.sem, 1)

            def divide(layer, i, par, n, u):
                g, half_ = divmod(u, T)
                v.wait_ge(pv_turned.sem, pv_turned.at(layer, i, n * UNITS + u + 1))
                src = p6[:, P:2 * P].rearrange("p (h c) -> p h c", h=GH)
                link(v.reciprocal(rden[:, :], src[:, :, HD]))
                dst = ao[:, par if layer == 0 else n, half_, g * 32:(g + 1) * 32].rearrange("p (h d) -> p h d", d=HD)
                v.tensor_tensor(dst, src[:, :, 0:HD], rden[:, :].unsqueeze(2).broadcast_to((P, GH, HD)),
                                ALU.mult).then_inc(divided.sem, 1)

            def take_logits(layer, i):
                v.wait_ge(logits_done.sem, logits_done.at(layer, i, 1))
                src = bank7(E)
                link(v.tensor_reduce(red[:, :], src, AX.X, ALU.max))
                link(v.tensor_tensor(logit[:, :, :], src, red[:, :].unsqueeze(2).broadcast_to((P, T, E)), ALU.subtract))
                close7()
                v.sem_inc(centred.sem, 1)

            def route(layer, i, par):
                v.wait_ge(exps_done.sem, exps_done.at(layer, i, 1))
                link(v.tensor_reduce(red[:, :], prob[:, :, :], AX.X, ALU.add))
                link(v.reciprocal(red2[:, :], red[:, :]))
                link(v.tensor_tensor(prob[:, :, :], prob[:, :, :], red2[:, :].unsqueeze(2).broadcast_to((P, T, E)), ALU.mult))
                if layer == 1:
                    link(v.tensor_reduce(red[:, :], prob[:, :, :], AX.X, ALU.max))
                    v.tensor_tensor(logit[:, :, :], prob[:, :, :], red[:, :].unsqueeze(2).broadcast_to((P, T, E)),
                                    ALU.subtract).then_inc(centred.sem, 1)
                for t in range(T):
                    other = prob[:, t, :].unsqueeze(1).broadcast_to((P, E, E))
                    own = prob[:, t, :].unsqueeze(2).broadcast_to((P, E, E))
                    v.tensor_tensor(cmp[:, t, :, :], other, own, ALU.is_gt)
                    last = v.tensor_tensor(cmp2[:, t, :, :], other, own, ALU.is_equal)
                link(last)
                lower = const[:, LOWER:LOWER + E * E].unsqueeze(1).broadcast_to((P, T, E * E))
                flat, flat2 = (c[:, :, :, :].rearrange("p t e j -> p t (e j)") for c in (cmp, cmp2))
                link(v.tensor_tensor(flat2, flat2, lower, ALU.mult))
                plus(flat, flat, flat2)
                link(v.tensor_reduce(sel[:, :, :], cmp[:, :, :, :], AX.X, ALU.add))
                link(v.tensor_scalar(sel[:, :, :], sel[:, :, :], 1.5, None, ALU.is_lt))
                if layer == 0:
                    v.tensor_tensor(gate[:, par], prob[:, :, :], sel[:, :, :], ALU.mult).then_inc(gates_ready.sem, 1)
                else:
                    v.wait_ge(exps_done.sem, exps_done.at(layer, i, 2))
                    link(v.tensor_tensor(gate[:, par], eprob[:, :, :], sel[:, :, :], ALU.mult))
                    link(v.tensor_reduce(red[:, :], gate[:, par], AX.X, ALU.add))
                    link(v.reciprocal(red2[:, :], red[:, :]))
                    v.tensor_tensor(gate[:, par], gate[:, par], red2[:, :].unsqueeze(2).broadcast_to((P, T, E)),
                                    ALU.mult).then_inc(gates_ready.sem, 1)
                v.wait_ge(gates_ready.sem, gates_ready.at(layer, i, 1))

            def add_expert(layer, i, par, e, sums):
                v.wait_ge(down_done.sem, down_done.at(layer, i, e + 1))
                for t in range(T):
                    last = v.scalar_tensor_tensor(sums[:, par, t, :], p7[:, t * D:(t + 1) * D], gate[:, par, t, e:e + 1],
                                                  sums[:, par, t, :], ALU.mult, ALU.add)
                link(last)
                close7()

            def add_product(done, layer, i, k, dst, other):
                v.wait_ge(done.sem, done.at(layer, i, k))
                plus(dst, other, bank7())
                close7()

            def batch(i):
                return X[:, bass.ds(i.times(T), T), :]

            def tiles_of(i):
                return [X[:, bass.ds(i.times(T, t), 1), :].rearrange("p t d -> p (t d)") for t in range(T)]

            def tiles(x_):
                return [x_[:, t, :] for t in range(T)]

            def extra(layer, s, x, f, b, nx, par, F_, A_, N_):
                at = (layer, s, x)
                odd = 1 - par
                if layer == 0:
                    if A_ and s < G - 1 and x < 2:
                        mask_spread(0, b, s + 1, x)
                    if F_ and at == (0, 0, 4):
                        add_product(o_proj, 0, f, 1, res[:, par], res[:, par])
                    if A_ and at == (0, 0, 5):
                        norm(tiles(xn), n1, 1e-5, "L0_ffn_g1", "L0_ffn_be1", n1_ready)
                    if A_ and at == (0, 1, 3):
                        add_product(mix_done, 0, b, 1, x1[:, :, :], n1[:, :, :])
                        plus(x1[:, :, :], x1[:, :, :], xn[:, :, :])
                        plus(x1[:, :, :], x1[:, :, :], row("L0_ffn_mix_b"))
                    if A_ and at == (0, 1, 5):
                        norm(tiles(x1), n1, 1e-5, "L0_ffn_g2", "L0_ffn_be2", hid_ready)
                        plus(res[:, odd], batch(b), row("L0_attn_bo"))
                        plus(res[:, odd], res[:, odd], x1[:, :, :])
                    if N_ and at == (0, 1, 6):
                        norm(tiles_of(nx), xn, 1e-5, done=xn_ready)
                    if A_ and at == (0, 2, 3):
                        take_logits(0, b)
                    if N_ and at == (0, 2, 5):
                        take_half(0, nx, par, 0, 0, full, bq, q_proj)
                    if A_ and at == (0, 2, 6):
                        route(0, b, odd)
                    if N_ and at == (0, 3, 0):
                        take_half(0, nx, par, 0, 1, full, bq, q_proj)
                        split(0, nx, par, 0, qs, 32, q_split)
                    if N_ and at == (0, 3, 1):
                        take_half(0, nx, par, 0, 0, full, bk, k_proj)
                    if N_ and at == (0, 3, 2):
                        take_half(0, nx, par, 0, 1, full, bk, k_proj)
                    if A_ and at == (0, 3, 4):
                        add_product(b2_done, 0, b, 1, res[:, odd], res[:, odd])
                    if N_ and at == (0, 3, 5):
                        take_v(0, nx, par, 0)
                    if N_ and at == (0, 3, 6):
                        mask_spread(0, nx, 0, 0)
                        mask_spread(0, nx, 0, 1)
                        link(v.tensor_copy(ks[0:96, par, :, :], full[0:96, :, :]))
                        link(v.tensor_tensor(ks[64:96, par, :, :], full[64:96, :, :], ks[64:96, par, :, :].bitcast(f32),
                                             ALU.subtract))
                        far_keys(par)
                        v.sem_inc(k_split.sem, 1)
                    if F_ and at == (0, 3, 6):
                        link(v.tensor_scalar(batch(f), res[:, par], 1.0, None, ALU.mult))
                    return
                if A_ and s == 0 and x in (0, 1):
                    take_half(1, b, odd, 1, x, full, bq, q_proj)
                    if x == 1:
                        split(1, b, odd, 1, qs, 32, q_split)
                if A_ and s == 0 and x in (4, 5):
                    take_half(1, b, odd, 1, x - 4, full, bk, k_proj)
                    if x == 5:
                        split(1, b, odd, 1, ks, 64, k_split)
                if A_ and at == (1, 0, 6):
                    take_v(1, b, odd, 1)
                if F_ and at == (1, 0, 3):
                    add_product(o_proj, 1, f, 2, res[:, par], res[:, par])
                if A_ and at == (1, 1, 2):
                    plus(res[:, odd], batch(b), row("L1_attn_bo"))
                    plus(x1[:, :, :], xn[:, :, :], row("L1_ffn_bo"))
                if N_ and at == (1, 1, 6):
                    norm(tiles_of(nx), xn, 1e-5, done=xn_ready)
                if N_ and s == 2 and x in (1, 4):
                    take_half(1, nx, par, 0, x // 4, full, bq, q_proj)
                    if x == 4:
                        split(1, nx, par, 0, qs, 32, q_split)
                if A_ and at == (1, 2, 3):
                    add_product(o_proj, 1, b, 1, x1[:, :, :], x1[:, :, :])
                    norm(tiles(x1), acc[:, odd], 1e-6, "L1_ffn_ln1_g", "L1_ffn_ln1_b", hid_ready)
                if A_ and at == (1, 2, 6):
                    take_logits(1, b)
                    route(1, b, odd)
                if N_ and s == 3 and x in (0, 1):
                    take_half(1, nx, par, 0, x, full, bk, k_proj)
                    if x == 1:
                        split(1, nx, par, 0, ks, 64, k_split)
                if A_ and at == (1, 3, 3):
                    add_product(b2_done, 1, b, 1, acc[:, odd], acc[:, odd])
                if N_ and at == (1, 3, 4):
                    take_v(1, nx, par, 0)
                if F_ and at == (1, 3, 6):
                    norm(tiles(acc[:, par]), n1, 1e-6, "L1_ffn_ln2_g", "L1_ffn_ln2_b")
                    v.tensor_tensor(batch(f), res[:, par], n1[:, :, :], ALU.add).then_inc(out_ready.sem, 1)
                    v.wait_ge(out_ready.sem, out_ready.at(1, f, 1))

            def iteration(layer, it, par, F_, A_, N_):
                f, b, nx, odd = it, it + 1, it + 2, 1 - par
                sums = res if layer == 0 else acc
                tail = [(f, par, layer, UNITS - 2), (f, par, layer, UNITS - 1)] if F_ else []
                for s in range(G):
                    def more(x):
                        extra(layer, s, x, f, b, nx, par, F_, A_, N_)

                    n, g = pairs_of(layer, s)[0]
                    more(0)
                    if layer == 0:
                        if A_:
                            partial_max(layer, b, n, T * g)
                        more(1)
                        if tail:
                            divide(layer, *tail[0])
                        if A_:
                            minus_max(layer, b, n, T * g)
                            partial_max(layer, b, n, T * g + 1)
                        more(2)
                        if tail:
                            divide(layer, *tail[1])
                        if A_:
                            minus_max(layer, b, n, T * g + 1)
                        more(3)
                        if F_:
                            add_expert(layer, f, par, 2 * s, sums)
                        more(4)
                        if F_:
                            add_expert(layer, f, par, 2 * s + 1, sums)
                        tail = [(b, odd, n, T * g), (b, odd, n, T * g + 1)] if A_ else []
                        more(5)
                        more(6)
                        continue
                    if A_:
                        partial_max(layer, b, n, T * g)
                    if tail:
                        divide(layer, *tail[0])
                    if A_:
                        minus_max(layer, b, n, T * g)
                        partial_max(layer, b, n, T * g + 1)
                    more(1)
                    if tail:
                        divide(layer, *tail[1])
                    if A_:
                        minus_max(layer, b, n, T * g + 1)
                    more(2)
                    tail = [(b, odd, n, T * g), (b, odd, n, T * g + 1)] if A_ else []
                    if F_:
                        add_expert(layer, f, par, 2 * s, sums)
                    n, g = pairs_of(layer, s)[1]
                    if A_:
                        partial_max(layer, b, n, T * g)
                    more(3)
                    if A_:
                        divide(layer, *tail[0])
                        minus_max(layer, b, n, T * g)
                        partial_max(layer, b, n, T * g + 1)
                    if F_:
                        add_expert(layer, f, par, 2 * s + 1, sums)
                    more(4)
                    if A_:
                        divide(layer, *tail[1])
                        minus_max(layer, b, n, T * g + 1)
                        tail = [(b, odd, n, T * g), (b, odd, n, T * g + 1)]
                    more(5)
                    more(6)

            run(v, [steps, roots], iteration)


LOOP_STEPS = [124, 162]
LOOP_ROOTS = [6, 6]
LOOP_BANK7 = [60, 54]

WEIGHTS_T = ["Wq", "Wk", "Wv", "Wo"]


def constants():
    import numpy as np
    c = np.zeros((P, NCONST), np.float32)
    p = np.arange(P)[:, None]
    c[:, EYE:EYE + P] = np.eye(P)
    c[:, RMASK:RMASK + L] = (np.arange(L)[None, :] % RHO) == p // HD
    c[:, HMASK:HMASK + GH] = (p % 32) // HD == np.arange(GH)[None, :]
    c[:16, EYE16:EYE16 + 16] = np.eye(16)
    c[:, LOWER:SPREAD] = (np.arange(E)[None, :] < np.arange(E)[:, None]).reshape(-1)
    row, col = p % 32, np.arange(P)[None, :] % HD
    for s in range(GH):
        c[:64, SPREAD + s * P:SPREAD + (s + 1) * P] = (row == s * HD + col)[:64]
    return c


def kernel(**inputs):
    import numpy as np
    import concourse.bacc as bacc
    from concourse.bass_utils import run_bass_kernel_spmd

    nc = bacc.Bacc("TRN2", target_bir_lowering=False, num_devices=1)
    arrays = {"const": constants(), "rows": np.stack([np.asarray(inputs[n]) for n in ROWS])}
    arrays["far"] = np.ascontiguousarray(np.asarray(inputs["L0_attn_dist_emb"])[[0, NPOS - 1]].T)
    for name, value in inputs.items():
        value = np.asarray(value)
        if name in ROWS:
            continue
        if name[:7] in ("L0_attn", "L1_attn") and name[8:] in WEIGHTS_T or name == "L0_attn_dist_emb":
            value = value.T
        if name[8:] in ("bq", "bk"):
            if name == "L0_attn_bq":
                arrays["bq_heads"] = np.ascontiguousarray(value.reshape(HEADS, HD).T)
            value = value.reshape(G, D // G).T
        if name in ("L0_ffn_b1", "L1_ffn_be1"):
            value = value.reshape(E * FT, P).T
        arrays[name] = np.ascontiguousarray(value)
    a = {n: nc.dram_tensor(f"in_{n}", v.shape, mybir.dt.from_np(v.dtype), kind="ExternalInput").ap() for n, v in arrays.items()}
    out = nc.dram_tensor("out_0", (B, L, D), mybir.dt.float32, kind="ExternalOutput").ap()
    build(nc, a, out)
    r = run_bass_kernel_spmd(nc, [{f"in_{n}": v for n, v in arrays.items()}], core_ids=[0])
    return r.results[0]["out_0"]
```

```python
from contextlib import ExitStack

import concourse.bass as bass
from concourse import mybir

B, L, D = 16, 256, 128
P = 128
T = L // P
HEADS, HD = 16, 8
LEFT, RIGHT = 64, 8
NPOS = LEFT + RIGHT + 1
E, F = 8, 512
FT = F // P
G, GH = 4, 4
UNITS = G * T
RHO = P // HD
ROWS = ["L0_attn_bv", "L0_attn_bo", "L0_ffn_g1", "L0_ffn_be1", "L0_ffn_mix_b", "L0_ffn_g2", "L0_ffn_be2",
        "L1_attn_bv", "L1_attn_bo", "L1_ffn_bo", "L1_ffn_ln1_g", "L1_ffn_ln1_b", "L1_ffn_ln2_g", "L1_ffn_ln2_b"]
ATTN = ["L0_attn", "L1_attn", "L1_ffn"]
EYE, RMASK, HMASK, EYE16, LOWER = 0, 128, 384, 388, 404
SPREAD = LOWER + E * E
NCONST = SPREAD + GH * P




class Batch:

    def __init__(self, c, j=None):
        self.c, self.j = c, j
        self.first = j is None and c == 0

    def __add__(self, n):
        return Batch(self.c + n, self.j)

    def times(self, n, k=0):
        fixed = self.c * n + k
        return fixed if self.j is None else self.j * (2 * n) + fixed


class Signal:

    def __init__(self, sem, layer0, layer1):
        self.sem, self.counts = sem, (layer0, layer1)

    def at(self, layer, i, k):
        return i.times(self.counts[layer], k + layer * B * self.counts[0])


class Tally:

    def __init__(self, per_loop):
        self.base, self.n, self.per_loop = 0, 0, per_loop

    def next(self):
        self.n += 1
        return self.base + self.n

    def enter(self, j):
        self.start = self.base + self.n
        self.base, self.n = j * self.per_loop[0] + self.start, 0

    def leave(self, loops, name):
        per = self.per_loop.pop(0)
        assert self.n == per, f"{name} {self.n} for {per}"
        self.base, self.n = self.start + loops * per, 0


FAR_LEFT = -(-(L // T + LEFT - 1) // RHO) * RHO
FAR_RIGHT = (P - RIGHT + 1) // RHO * RHO

LOOPS = B // 2 - 1


def build(nc, a, out):
    f32, f32r = mybir.dt.float32, mybir.dt.float32r
    ALU, ACT, AX = mybir.AluOpType, mybir.ActivationFunctionType, mybir.AxisListType
    SCALE = float(HD) ** -0.5
    ctx = ExitStack()
    with ctx:
        def sb(name, shape, dt=f32):
            return ctx.enter_context(nc.sbuf_tensor(name, shape, dt))

        def signal(name, layer0=0, layer1=0):
            return Signal(ctx.enter_context(nc.semaphore(name)), layer0, layer1)

        X = sb("X", [P, B * T, D])
        const = sb("const", [P, NCONST])
        rows = sb("rows", [P, len(ROWS), D])
        eye = const[:, EYE:EYE + P]
        rmask = const[:, RMASK:RMASK + L]
        spread = sb("spread", [P, GH, P], f32r)
        wq = sb("wq", [P, 3, G, P])
        wk = sb("wk", [P, 3, G, P])
        wv = sb("wv", [P, 3, D])
        wo = sb("wo", [P, 3, D])
        bq = sb("bq", [P, 2, G])
        bk = sb("bk", [P, 2, G])
        mixw = sb("mixw", [P, D])
        rw = sb("rw", [P, 2, E])
        w1 = sb("w1", [P, E, F])
        w2 = sb("w2", [P, E, FT, D])
        b1 = sb("b1", [P, 2, E, FT])
        b2 = sb("b2", [E, 2, D])
        ext = sb("ext", [HD, 512])
        toep = sb("toep", [P, 496])
        ones16 = sb("ones16", [RHO, P], f32r)
        half = sb("half", [P, T])
        idle = sb("idle", [P, 1])

        xn = sb("xn", [P, 2, T, D])
        stats = sb("stats", [P, T, 6])
        mv = sb("mv", [P, T, 2])
        ve = sb("ve", [P, T])
        rstd = sb("rstd", [P, T])
        xT = sb("xT", [P, L])
        n1T = sb("n1T", [P, L])
        hidT = sb("hidT", [P, 2, L])
        q_full = sb("q_full", [P, G, L])
        k_full = sb("k_full", [P, G, L])
        far_full = sb("far_full", [P, G, L])
        qs = sb("qs", [P, 2, G, L], f32r)
        ks = sb("ks", [P, 2, G, L], f32r)
        qm = sb("qm", [P, 2, GH, L], f32r)
        qx = sb("qx", [P, 2, GH, L])
        vp = sb("vp", [P, 2, T, HEADS, 32])
        pm = sb("pm", [P, 32])
        pm2 = sb("pm2", [P, 2, 16])
        nm = sb("nm", [16, 2, 32])
        ksa = sb("ksa", [P, 2, G, L], f32r)
        far = sb("far", [P, T])
        shift = sb("shift", [16, 2, 16, 32], f32r)
        probs = sb("probs", [P, 2, T, GH * P])
        pv = sb("pv", [P, P])
        rden = sb("rden", [P, GH])
        ao = sb("ao", [P, 2, T, D])
        aoT = sb("aoT", [P, L])
        n1 = sb("n1", [P, T, D])
        x1 = sb("x1", [P, T, D])
        acc = sb("acc", [P, 2, T, D])
        res = sb("res", [P, 2, T, D])
        hT = sb("hT", [P, 2, FT, L])
        logit = sb("logit", [P, T, E])
        prob = sb("prob", [P, T, E])
        eprob = sb("eprob", [P, T, E])
        red = sb("red", [P, T])
        red2 = sb("red2", [P, T])
        cmp = sb("cmp", [P, T, E, E])
        cmp2 = sb("cmp2", [P, T, E, E])
        sel = sb("sel", [P, T, E])
        gate = sb("gate", [P, 2, T, E])
        gT = sb("gT", [E, L])

        score = [ctx.enter_context(nc.psum_tensor(f"score{n}", [P, 1024], f32)) for n in range(2)]
        p4, p5, p6, p7 = [ctx.enter_context(nc.psum_tensor(f"bank{n}", [P, 512], f32)) for n in range(4, 8)]

        loaded, x_loaded, loaded1, weights0, weights1, shifts_loaded, stored, ext_ready, ready = (
            ctx.enter_context(nc.semaphore(n)) for n in
            ("loaded", "x_loaded", "loaded1", "weights0", "weights1", "shifts_loaded", "stored", "ext_ready", "ready"))
        dve = signal("dve")
        small_read = signal("small_read")
        down_read = signal("down_read")
        var_ready = signal("var_ready")
        rstd_ready = signal("rstd_ready")
        normed = signal("normed", 2, 1)
        gained = signal("gained", 2, 1)
        xn_ready = signal("xn_ready", 1, 1)
        n1_ready = signal("n1_ready", 1, 0)
        hid_ready = signal("hid_ready", 1, 1)
        xn_turned = signal("xn_turned", 1, 1)
        n1_turned = signal("n1_turned", 1, 0)
        hid_turned = signal("hid_turned", 1, 1)
        ao_turned = signal("ao_turned", 1, 2)
        xT_out = signal("xT_out", 1, 1)
        n1T_out = signal("n1T_out", 1, 0)
        hidT_out = signal("hidT_out", 1, 1)
        aoT_out = signal("aoT_out", 1, 2)
        q_proj = signal("q_proj", 2, 4)
        k_proj = signal("k_proj", 2, 4)
        v_proj = signal("v_proj", 1, 2)
        q_taken = signal("q_taken", 2, 4)
        k_taken = signal("k_taken", 2, 4)
        q_split = signal("q_split", 1, 2)
        k_split = signal("k_split", 1, 2)
        near_split = signal("near_split", 1, 0)
        far_taken = signal("far_taken", 1, 0)
        v_ready = signal("v_ready", 1, 2)
        q_masked = signal("q_masked", G, 2 * G)
        qx_proj = signal("qx_proj", 2 * G, 0)
        qx_out = signal("qx_out", 2 * G, 0)
        scores_ready = signal("scores_ready", UNITS, 2 * UNITS)
        part_max = signal("part_max", UNITS, 2 * UNITS)
        max_turned = signal("max_turned", UNITS, 2 * UNITS)
        nm_ready = signal("nm_ready", UNITS, 2 * UNITS)
        shift_rows = signal("shift_rows", UNITS, 2 * UNITS)
        shifted = signal("shifted", UNITS, 2 * UNITS)
        probs_ready = signal("probs_ready", UNITS, 2 * UNITS)
        pv_done = signal("pv_done", UNITS, 2 * UNITS)
        pv_out = signal("pv_out", UNITS, 2 * UNITS)
        pv_turned = signal("pv_turned", UNITS, 2 * UNITS)
        divided = signal("divided", UNITS, 2 * UNITS)
        o_proj = signal("o_proj", 1, 2)
        mix_done = signal("mix_done", 1, 0)
        logits_done = signal("logits_done", 1, 1)
        centred = signal("centred", 1, 2)
        exps_done = signal("exps_done", 1, 2)
        gates_ready = signal("gates_ready", 1, 1)
        gates_turned = signal("gates_turned", 1, 1)
        gates_out = signal("gates_out", 1, 1)
        b2_done = signal("b2_done", 1, 1)
        up_done = signal("up_done", 2 * E, 2 * E)
        act_done = signal("act_done", 2 * E, 2 * E)
        down_done = signal("down_done", E, E)
        out_ready = signal("out_ready", 0, 1)

        small = (p5, p7)
        up_banks = ((p4, p4), (p4, p5))

        def row(name):
            return rows[:, ROWS.index(name), :].unsqueeze(1).broadcast_to((P, T, D))

        def attention(layer, i_par, n):
            return (0, i_par) if layer == 0 else ((2, 0), (1, 1))[n]

        def pairs_of(layer, s):
            return [(0, s)] if layer == 0 else [(s // 2, 2 * (s % 2)), (s // 2, 2 * (s % 2) + 1)]

        def following(layer, n, g):
            if g + 1 < G:
                return 0, n, g + 1
            return (0, 1, 0) if layer == 1 and n == 0 else (1, 0, 0)

        def run(eng, tallies, iteration):
            for layer in range(2):
                iteration(layer, Batch(-2), 0, False, False, True)
                iteration(layer, Batch(-1), 1, False, True, True)
                with eng.Fori(0, LOOPS) as j:
                    for t in tallies:
                        t.enter(j)
                    iteration(layer, Batch(0, j), 0, True, True, True)
                    iteration(layer, Batch(1, j), 1, True, True, True)
                for name, t in zip("abc", tallies):
                    t.leave(LOOPS, f"layer {layer} {name}")
                iteration(layer, Batch(B - 2), 0, True, True, False)
                iteration(layer, Batch(B - 1), 1, True, False, False)

        counts = {}
        block = ctx.enter_context(nc.Block())

        @block.sync
        def _(sp):
            def load(sem, dst, src):
                sp.dma_start(dst, src).then_inc(sem, 16)
                counts[sem] = counts.get(sem, 0) + 16

            def experts(layer, sem):
                names = (("w1", "w2"), ("We1", "We2"))[layer]
                load(sem, w1[:, :, :], a[f"L{layer}_ffn_{names[0]}"].rearrange("e p f -> p e f"))
                load(sem, w2[:, :, :, :].rearrange("p e t d -> p (e t) d"),
                     a[f"L{layer}_ffn_{names[1]}"].rearrange("e (t p) d -> p (e t) d", p=P))

            x = a["L0_attn_hidden_states"].rearrange("b (t p) d -> p (b t) d", p=P)
            load(loaded, far[:, :], a["far"])
            sp.dma_start(ext[:, 192:192 + NPOS], a["L0_attn_dist_emb"]).then_inc(shifts_loaded, 16)
            load(loaded, const[:, :], a["const"])
            load(loaded, X[:, 0:T, :], x[:, 0:T, :])
            load(loaded, rows[:, :, :], a["rows"].partition_broadcast(P))

            def attention_weights(sem, n):
                name = ATTN[n]
                for w, key in ((wq, "Wq"), (wk, "Wk")):
                    load(sem, w[:, n, :, :].rearrange("p g c -> p (g c)"), a[f"{name}_{key}"])
                load(sem, wv[:, n, :], a[f"{name}_Wv"])
                load(sem, wo[:, n, :], a[f"{name}_Wo"])
                if n < 2:
                    for b, key in ((bq, "bq"), (bk, "bk")):
                        load(sem, b[:, n, :], a[f"{name}_{key}"])

            def expert_vectors(sem, n):
                r, bu, bd = (("router_w", "b1", "b2"), ("Wr", "be1", "be2"))[n]
                load(sem, rw[:, n, :], a[f"L{n}_ffn_{r}"])
                load(sem, b1[:, n, :, :].rearrange("p e t -> p (e t)"), a[f"L{n}_ffn_{bu}"])
                load(sem, b2[:, n, :], a[f"L{n}_ffn_{bd}"])

            attention_weights(loaded, 0)
            expert_vectors(loaded, 0)
            load(loaded, mixw[:, :], a["L0_ffn_mix_w"])
            sp.wait_ge(ext_ready, 2)
            for r in range(RHO):
                sp.dma_start(toep[HD * r:HD * r + HD, :], ext[:, 16 - r:16 - r + 496]).then_inc(shifts_loaded, 16)
            load(x_loaded, X[:, T:, :], x[:, T:, :])
            experts(0, weights0)
            attention_weights(loaded1, 1)
            attention_weights(loaded1, 2)
            expert_vectors(loaded1, 1)
            sp.wait_ge(down_done.sem, down_done.at(0, Batch(B - 1), E))
            experts(1, weights1)
            y = out.rearrange("b (t p) d -> b p t d", p=P)
            with sp.Fori(0, B) as i:
                sp.wait_ge(out_ready.sem, i + 1)
                sp.dma_start(y[bass.ds(i, 1)].rearrange("b p t d -> p (b t) d"), X[:, bass.ds(i * T, T), :]).then_inc(stored, 16)
            sp.wait_ge(stored, 16 * B)

        @block.gpsimd
        def _(pool):
            pool.memset(half[:, :], -0.5).then_inc(ready, 1)
            pool.memset(ones16[:, :].bitcast(f32), 1.0).then_inc(ready, 1)
            pool.memset(vp[:, :, :, :, :], 0.0).then_inc(ready, 1)
            pool.wait_ge(ready, 3)
            pool.memset(vp[:, :, :, :, HD:HD + 1], 1.0).then_inc(ready, 1)
            pool.wait_ge(loaded, counts[loaded])
            pool.tensor_copy(spread[:, :, :], const[:, SPREAD:].rearrange("p (h c) -> p h c", h=GH)).then_inc(ready, 1)
            pool.wait_ge(ready, 5)
            roots = Tally(LOOP_ROOTS[:])

            def root():
                value = roots.next()
                pool.wait_ge(var_ready.sem, value)
                pool.tensor_tensor(rstd[:, :], ve[:, :], half[:, :], ALU.pow).then_inc(rstd_ready.sem, 1)
                pool.wait_ge(rstd_ready.sem, value)

            def gain(layer, i, k, dst, g, add, done):
                pool.wait_ge(normed.sem, normed.at(layer, i, k))
                pool.tensor_tensor(dst, dst, row(g), ALU.mult).then_inc(gained.sem, 1)
                pool.wait_ge(gained.sem, gained.at(layer, i, k))
                pool.tensor_tensor(dst, dst, row(add), ALU.add).then_inc(done.sem, 1)
                pool.wait_ge(done.sem, done.at(layer, i, 1))

            def mask(layer, i, par, n, g):
                _, set_ = attention(layer, par, n)
                if g == 0:
                    pool.wait_ge(q_split.sem, q_split.at(layer, i, n + 1))
                if not (i.first and n == 0 and g < 2 and layer == 0):
                    pool.wait_ge(scores_ready.sem, scores_ready.at(layer, i, T * (n * G + g - 1)))
                pool.tensor_tensor(qm[0:96, g % 2, :, :],
                                   qs[0:96, set_, g, :].bitcast(f32).unsqueeze(1).broadcast_to((96, GH, L)),
                                   const[0:96, HMASK:HMASK + GH].unsqueeze(2).broadcast_to((96, GH, L)),
                                   ALU.mult).then_inc(q_masked.sem, 1)
                pool.wait_ge(q_masked.sem, q_masked.at(layer, i, n * G + g + 1))

            def low_parts(layer, i, par, n, whole, parts, lo, taken, done):
                _, set_ = attention(layer, par, n)
                pool.wait_ge(taken.sem, taken.at(layer, i, 2 * n + 2))
                last = pool.tensor_tensor(parts[lo:lo + 32, set_, :, :], whole[lo:lo + 32, :, :],
                                          parts[lo:lo + 32, set_, :, :].bitcast(f32), ALU.subtract)
                if layer == 0 and parts is ks:
                    last.then_inc(near_split.sem, 1)
                    pool.wait_ge(near_split.sem, near_split.at(0, i, 1))
                    pool.wait_ge(far_taken.sem, far_taken.at(0, i, 1))
                    last = pool.tensor_tensor(ksa[64:96, set_, :, :], far_full[64:96, :, :],
                                              ksa[64:96, set_, :, :].bitcast(f32), ALU.subtract)
                last.then_inc(done.sem, 1)
                pool.wait_ge(done.sem, done.at(layer, i, n + 1))

            def iteration(layer, it, par, F_, A_, N_):
                b, nx, odd = it + 1, it + 2, 1 - par
                for s in range(G):
                    ahead = [] if not A_ else [following(layer, n, g) for n, g in pairs_of(layer, s)]
                    ahead = [(n2, g2) for on, n2, g2 in ahead if not on]
                    if ahead:
                        mask(layer, b, odd, *ahead[0])
                    if layer == 1 and s == 0 and A_:
                        low_parts(1, b, odd, 1, q_full, qs, 32, q_taken, q_split)
                    if layer == 1 and s == 1 and A_:
                        low_parts(1, b, odd, 1, k_full, ks, 64, k_taken, k_split)
                    if len(ahead) > 1:
                        mask(layer, b, odd, *ahead[1])
                    if layer == 1:
                        if s == 2 and N_:
                            low_parts(1, nx, par, 0, q_full, qs, 32, q_taken, q_split)
                        if s == 2 and A_:
                            root()
                            gain(1, b, 1, acc[:, odd], "L1_ffn_ln1_g", "L1_ffn_ln1_b", hid_ready)
                        if s == 3 and N_:
                            low_parts(1, nx, par, 0, k_full, ks, 64, k_taken, k_split)
                            mask(1, nx, par, 0, 0)
                        if s == 3 and F_:
                            root()
                    elif s < 2 and A_:
                        root()
                        gain(0, b, s + 1, n1[:, :, :], *(("L0_ffn_g1", "L0_ffn_be1", n1_ready),
                                                         ("L0_ffn_g2", "L0_ffn_be2", hid_ready))[s])
                    if s == 0 and N_:
                        root()
                if N_ and layer == 0:
                    low_parts(0, nx, par, 0, q_full, qs, 32, q_taken, q_split)
                if N_ and layer == 0:
                    mask(0, nx, par, 0, 0)
                if N_ and layer == 0:
                    low_parts(0, nx, par, 0, k_full, ks, 64, k_taken, k_split)

            run(pool, [roots], iteration)

        @block.scalar
        def _(act):
            act.wait_ge(loaded, counts[loaded])
            act.wait_ge(ready, 5)

            def take(turned, out_, layer, i, k, dst, rows_=P):
                act.wait_ge(turned.sem, turned.at(layer, i, k))
                act.activation(dst, small[layer][0:rows_, 0:L], ACT.Copy).then_inc(out_.sem, 1)
                act.wait_ge(out_.sem, out_.at(layer, i, k))
                act.sem_inc(small_read.sem, 1)

            def take_half(layer, i, par, n, pair, dst, bias, proj, taken, done):
                which, set_ = attention(layer, par, n)
                act.wait_ge(proj.sem, proj.at(layer, i, 2 * n + pair + 1))
                if not (i.first and layer == 0 and n == 0):
                    act.wait_ge(done.sem, done.at(layer, i, n))
                lo, parts = (32, qs) if dst is q_full else (64, ks)
                for g in (2 * pair, 2 * pair + 1):
                    whole = slice(0, 96) if which == 0 and dst is k_full else slice(lo, lo + 32)
                    for rows_, to in ((whole, dst[whole, g, :]), (slice(0, 96), parts[0:96, set_, g, :])):
                        src = small[layer][rows_, (g % 2) * L:(g % 2 + 1) * L]
                        if which < 2:
                            last = act.activation(to, src, ACT.Identity, bias=bias[rows_, which, g:g + 1])
                        else:
                            last = act.activation(to, src, ACT.Copy)
                last.then_inc(taken.sem, 1)
                act.wait_ge(taken.sem, taken.at(layer, i, 2 * n + pair + 1))
                act.sem_inc(small_read.sem, 1)

            def take_q(layer, i, par, n, pair):
                take_half(layer, i, par, n, pair, q_full, bq, q_proj, q_taken, q_split)

            def take_k(layer, i, par, n, pair):
                take_half(layer, i, par, n, pair, k_full, bk, k_proj, k_taken, k_split)

            def take_v(i):
                act.wait_ge(v_proj.sem, v_proj.at(1, i, 1))
                for t in range(T):
                    last = act.activation(vp[:, 0, t, :, 0:HD], p7[:, t * D:(t + 1) * D].rearrange("p (h d) -> p h d", d=HD),
                                          ACT.Copy)
                last.then_inc(v_ready.sem, 1)
                act.wait_ge(v_ready.sem, v_ready.at(1, i, 1))
                act.sem_inc(small_read.sem, 1)

            def hidden(layer, i, e, pair):
                act.wait_ge(up_done.sem, up_done.at(layer, i, 2 * e + pair + 1))
                for ft in (2 * pair, 2 * pair + 1):
                    last = act.activation(hT[:, e % 2, ft, :], up_banks[layer][pair][:, (ft % 2) * L:(ft % 2 + 1) * L],
                                          (ACT.Silu, ACT.Gelu)[layer], bias=b1[:, layer, e, ft:ft + 1])
                last.then_inc(act_done.sem, 1)

            def load_table(experts):
                if experts:
                    act.activation(idle[:, :], half[:, 0:1], ACT.Silu)

            def exp(layer, i, n, u):
                act.wait_ge(shifted.sem, shifted.at(layer, i, n * UNITS + u + 1))
                act.activation(probs[:, u % 2, :, :].rearrange("p t c -> p (t c)"), score[u % 2][:, :], ACT.Exp,
                               scale=SCALE).then_inc(probs_ready.sem, 1)

            def take_values(layer, i, k):
                act.wait_ge(pv_done.sem, pv_done.at(layer, i, k))
                act.activation(pv[:, :], p6[:, 0:P], ACT.Copy).then_inc(pv_out.sem, 1)

            def centre_exp(layer, i, k, src, dst):
                act.wait_ge(centred.sem, centred.at(layer, i, k))
                act.activation(dst[:, :, :], src[:, :, :], ACT.Exp).then_inc(exps_done.sem, 1)

            def extra(layer, s, x, f, b, nx, par, F_, A_, N_):
                at = (layer, s, x)
                if F_ and at == (0, 0, 3):
                    take(ao_turned, aoT_out, 0, f, 1, aoT[:, :])
                if F_ and at == (1, 0, 2):
                    take(ao_turned, aoT_out, 1, f, 2, aoT[:, :])
                if A_ and at == (0, 1, 2):
                    take(n1_turned, n1T_out, 0, b, 1, n1T[:, :])
                if A_ and at in ((0, 2, 2), (1, 3, 1)):
                    take(hid_turned, hidT_out, layer, b, 1, hidT[:, 1 - par, :])
                if A_ and at == (1, 2, 2):
                    take(ao_turned, aoT_out, 1, b, 1, aoT[:, :])
                if A_ and at == (0, 2, 4):
                    centre_exp(0, b, 1, logit, prob)
                if A_ and at == (1, 3, 3):
                    centre_exp(1, b, 1, logit, prob)
                if A_ and at == (1, 3, 4):
                    centre_exp(1, b, 2, logit, eprob)
                if A_ and at == (0, 3, 2):
                    take(gates_turned, gates_out, 0, b, 1, gT[:, :], E)
                if F_ and at == (1, 1, 3):
                    take(gates_turned, gates_out, 1, f, 1, gT[:, :], E)
                if N_ and at in ((0, 1, 4), (1, 1, 2)):
                    take(xn_turned, xT_out, layer, nx, 1, xT[:, :])
                if N_ and at in ((0, 1, 5), (0, 2, 4)):
                    take_q(0, nx, par, 0, s - 1)
                if N_ and at in ((0, 2, 5), (0, 3, 0)):
                    take_k(0, nx, par, 0, s - 2)
                if A_ and layer == 1 and s == 0 and x in (0, 1):
                    take_q(1, b, 1 - par, 1, x)
                if A_ and at in ((1, 0, 6), (1, 1, 0)):
                    take_k(1, b, 1 - par, 1, s)
                if N_ and at == (1, 3, 4):
                    take_v(nx)
                if N_ and layer == 1 and s == 2 and x in (0, 1):
                    take_q(1, nx, par, 0, x)
                if N_ and at in ((1, 2, 6), (1, 3, 0)):
                    take_k(1, nx, par, 0, s - 2)

            def iteration(layer, it, par, F_, A_, N_):
                f, b, nx = it, it + 1, it + 2
                if layer == 1 and not A_ and not F_:
                    act.wait_ge(loaded1, counts[loaded1])
                for s in range(G):
                    def more(x):
                        extra(layer, s, x, f, b, nx, par, F_, A_, N_)
                    n, g = pairs_of(layer, s)[0]
                    k = T * (n * G + g)
                    tail = A_ if s else F_
                    if layer == 1 and tail:
                        take_values(layer, b, k - 1)
                    if F_:
                        hidden(layer, f, 2 * s, 0)
                    if layer == 0:
                        more(0)
                    if layer == 1:
                        more(0)
                    if F_:
                        hidden(layer, f, 2 * s, 1)
                    if layer == 0 and tail:
                        take_values(layer, b, k - 1)
                    if layer == 0:
                        more(1)
                    if F_:
                        hidden(layer, f, 2 * s + 1, 0)
                    if tail:
                        take_values(layer, b, k)
                    if layer == 1:
                        more(1)
                    else:
                        more(2)
                    if F_:
                        hidden(layer, f, 2 * s + 1, 1)
                    if layer == 0:
                        more(3)
                    if A_:
                        exp(layer, b, n, T * g)
                    if layer == 0:
                        more(4)
                    if A_:
                        exp(layer, b, n, T * g + 1)
                    if layer == 1:
                        more(2)
                    if layer == 0:
                        more(5)
                        more(6)
                        load_table(F_ or A_)
                        continue
                    more(3)
                    n, g = pairs_of(layer, s)[1]
                    if A_:
                        take_values(layer, b, k + 1)
                        take_values(layer, b, k + 2)
                        exp(layer, b, n, T * g)
                    if A_:
                        exp(layer, b, n, T * g + 1)
                    more(4)
                    more(5)
                    more(6)

            run(act, [], iteration)

        @block.tensor
        def _(pe):
            pe.wait_ge(loaded, counts[loaded])
            pe.wait_ge(ready, 5)
            reads = {small_read: Tally(LOOP_SMALL[:]), down_read: Tally(LOOP_DOWN[:])}
            held, pe_layer = {}, [0]

            def open_bank(kind):
                for k in list(held):
                    if k is kind or pe_layer[0]:
                        pe.wait_ge(k.sem, held.pop(k)())
                t = reads[kind]
                t.next()
                held[kind] = lambda: t.base + t.n

            def turn(src, turned, rows_=P):
                open_bank(small_read)
                for t in range(T):
                    last = pe.transpose(small[pe_layer[0]][0:rows_, t * P:(t + 1) * P], src[:, t, :], eye)
                last.then_inc(turned.sem, 1)

            def by_token(lhs, w, done):
                open_bank(small_read)
                c = w.shape[-1]
                for t in range(T):
                    last = pe.matmul(small[pe_layer[0]][:, t * c:(t + 1) * c], lhs[:, t * P:(t + 1) * P], w, start=True, stop=True)
                last.then_inc(done.sem, 1)

            def project(w, n, pair, done):
                open_bank(small_read)
                for g in (2 * pair, 2 * pair + 1):
                    last = pe.matmul(small[pe_layer[0]][:, (g % 2) * L:(g % 2 + 1) * L], w[:, n, g, :], xT[:, :], start=True, stop=True)
                last.then_inc(done.sem, 1)

            def spread_queries(layer, i, par, g, pair):
                open_bank(small_read)
                for h in range(2):
                    last = pe.matmul(small[0][:, h * L:(h + 1) * L], spread[0:64, 2 * pair + h, :], qs[0:64, par, g, :],
                                     start=True, stop=True)
                last.then_inc(qx_proj.sem, 1)

            def scores(layer, i, par, n, u, tiles_=(0, 1)):
                g, half_ = divmod(u, T)
                _, set_ = attention(layer, par, n)
                k = n * UNITS + u + 1
                if tiles_[0] == 0 and not (i.first and layer == 0 and k <= 2):
                    pe.wait_ge(probs_ready.sem, probs_ready.at(layer, i, k - 2))
                if half_ == 0 and tiles_[0] == 0:
                    pe.wait_ge(q_masked.sem, q_masked.at(layer, i, n * G + g + 1))
                    if g == 0:
                        pe.wait_ge(k_split.sem, k_split.at(layer, i, n + 1))
                    if layer == 0:
                        pe.wait_ge(qx_out.sem, qx_out.at(layer, i, 2 * g + 2))
                for kb in tiles_:
                    dst = score[u % 2][:, kb * 512:(kb + 1) * 512]
                    keys = ks[0:96, set_, g, kb * P:(kb + 1) * P]
                    view = dst.rearrange("p (h l) -> p h l", h=GH)
                    if layer == 1 or kb == half_:
                        last = pe.matmul(dst, keys, qm[0:96, g % 2, :, half_ * P:(half_ + 1) * P], start=True, stop=layer == 1)
                        near = (0, P)
                    else:
                        near = (0, P - (L - FAR_LEFT)) if kb == 0 else (FAR_RIGHT, P)
                        for (lo, hi), stationary, start in ((near, keys, True),
                                                            (((near[1], P) if kb == 0 else (0, near[0])),
                                                             ksa[0:96, set_, g, kb * P:(kb + 1) * P], False)):
                            last = pe.matmul(view[:, :, lo:hi], stationary,
                                             qm[0:96, g % 2, :, half_ * P + lo:half_ * P + hi], start=start, stop=True,
                                             skip_group_check=True)
                    if layer == 0:
                        for m in range(near[0] // RHO, near[1] // RHO):
                            l0 = half_ * P + m * RHO
                            at = kb * P - l0 + 240
                            last = pe.matmul(view[:, :, m * RHO:(m + 1) * RHO], toep[:, at:at + P],
                                             qx[:, g % 2, :, l0:l0 + RHO], start=False, stop=m == near[1] // RHO - 1,
                                             skip_group_check=kb != half_)
                if tiles_[-1] == T - 1:
                    last.then_inc(scores_ready.sem, 1)

            def turn_max(layer, i, n, u):
                k = n * UNITS + u + 1
                pe.wait_ge(part_max.sem, part_max.at(layer, i, k))
                if not (i.first and layer == 0 and k <= 2):
                    pe.wait_ge(divided.sem, divided.at(layer, i, k - 2))
                pe.transpose(p6[0:16, 256:256 + P], pm2[:, u % 2, :], eye).then_inc(max_turned.sem, 1)

            def subtract(layer, i, n, u):
                pe.wait_ge(shift_rows.sem, shift_rows.at(layer, i, n * UNITS + u + 1))
                for kb in range(T):
                    last = pe.matmul(score[u % 2][:, kb * 512:(kb + 1) * 512], ones16[:, :],
                                     shift[:, u % 2, :, :].rearrange("p a b -> p (a b)"), start=False, stop=True,
                                     skip_group_check=True)
                last.then_inc(shifted.sem, 1)

            def values(layer, i, par, n, u, last_batch):
                _, set_ = attention(layer, par, n)
                g = u // T
                k = n * UNITS + u + 1
                pe.wait_ge(probs_ready.sem, probs_ready.at(layer, i, k))
                if last_batch and k == (1 + layer) * UNITS:
                    pe.wait_ge(divided.sem, divided.at(layer, i, k - 1))
                else:
                    pe.wait_ge(nm_ready.sem, nm_ready.at(layer, i, k + 1))
                if u == 0:
                    pe.wait_ge(v_ready.sem, v_ready.at(layer, i, n + 1))
                for kb in range(T):
                    for h in range(GH):
                        last = pe.matmul(p6[32 * h:32 * h + 32, 0:P], vp[:, set_, kb, g * GH + h, :],
                                         probs[:, u % 2, kb, h * P:(h + 1) * P], start=kb == 0, stop=kb == T - 1)
                last.then_inc(pv_done.sem, 1)

            def turn_values(layer, i, par, n, u):
                pe.wait_ge(pv_out.sem, pv_out.at(layer, i, n * UNITS + u + 1))
                pe.transpose(p6[:, P:2 * P], pv[:, :], eye).then_inc(pv_turned.sem, 1)

            def extra(layer, s, x, f, b, nx, par, F_, A_, N_):
                at = (layer, s, x)
                odd = 1 - par

                def take_in(ready_, i, k, src, turned, rows_=P):
                    pe.wait_ge(ready_.sem, ready_.at(layer, i, k))
                    turn(src, turned, rows_)

                def product(out_, i, k, lhs, w, done):
                    pe.wait_ge(out_.sem, out_.at(layer, i, k))
                    by_token(lhs, w, done)

                if layer == 0:
                    if A_ and s < G - 1 and x < 2:
                        spread_queries(0, b, odd, s + 1, x)
                    if F_ and at == (0, 0, 3):
                        take_in(divided, f, UNITS, ao[:, par], ao_turned)
                    if F_ and at == (0, 0, 4):
                        product(aoT_out, f, 1, aoT, wo[:, 0, :], o_proj)
                    if A_ and at == (0, 1, 2):
                        take_in(n1_ready, b, 1, n1, n1_turned)
                    if A_ and at == (0, 1, 3):
                        product(n1T_out, b, 1, n1T, mixw[:, :], mix_done)
                    if A_ and at == (0, 2, 2):
                        take_in(hid_ready, b, 1, n1, hid_turned)
                    if A_ and at == (0, 2, 3):
                        product(hidT_out, b, 1, hidT[:, odd, :], rw[:, 0, :], logits_done)
                    if N_ and at == (0, 1, 4):
                        take_in(xn_ready, nx, 1, xn[:, par], xn_turned)
                    if N_ and at in ((0, 1, 5), (0, 2, 4)):
                        pe.wait_ge(xT_out.sem, xT_out.at(0, nx, 1))
                        project(wq, 0, s - 1, q_proj)
                    if N_ and at in ((0, 2, 5), (0, 3, 0)):
                        project(wk, 0, s - 2, k_proj)
                    if N_ and at == (0, 3, 1):
                        by_token(xT, wv[:, 0, :], v_proj)
                    if N_ and at == (0, 3, 3):
                        pe.wait_ge(q_split.sem, q_split.at(0, nx, 1))
                        spread_queries(0, nx, par, 0, 0)
                    if A_ and at == (0, 3, 2):
                        take_in(gates_ready, b, 1, gate[:, odd], gates_turned, E)
                    if A_ and at == (0, 3, 4):
                        product(gates_out, b, 1, gT, b2[:, 0, :], b2_done)
                    if N_ and at == (0, 3, 5):
                        spread_queries(0, nx, par, 0, 1)
                    return
                if A_ and s == 0 and x in (0, 1):
                    project(wq, 1, x, q_proj)
                if A_ and at in ((1, 0, 6), (1, 1, 0)):
                    project(wk, 1, s, k_proj)
                if A_ and at == (1, 1, 1):
                    by_token(xT, wv[:, 1, :], v_proj)
                if F_ and at == (1, 0, 2):
                    take_in(divided, f, 2 * UNITS, ao[:, 1], ao_turned)
                if F_ and at == (1, 0, 3):
                    product(aoT_out, f, 2, aoT, wo[:, 1, :], o_proj)
                if N_ and at == (1, 1, 2):
                    take_in(xn_ready, nx, 1, xn[:, par], xn_turned)
                if N_ and s == 2 and x in (0, 1):
                    pe.wait_ge(xT_out.sem, xT_out.at(1, nx, 1))
                    project(wq, 2, x, q_proj)
                if A_ and at == (1, 2, 2):
                    take_in(divided, b, UNITS, ao[:, 0], ao_turned)
                if A_ and at == (1, 2, 3):
                    product(aoT_out, b, 1, aoT, wo[:, 2, :], o_proj)
                if N_ and at in ((1, 2, 6), (1, 3, 0)):
                    project(wk, 2, s - 2, k_proj)
                if A_ and at == (1, 3, 1):
                    take_in(hid_ready, b, 1, acc[:, odd], hid_turned)
                if A_ and at == (1, 3, 2):
                    product(hidT_out, b, 1, hidT[:, odd, :], rw[:, 1, :], logits_done)
                if N_ and at == (1, 3, 4):
                    by_token(xT, wv[:, 2, :], v_proj)
                if F_ and at == (1, 1, 3):
                    take_in(gates_ready, f, 1, gate[:, par], gates_turned, E)
                if F_ and at == (1, 1, 6):
                    product(gates_out, f, 1, gT, b2[:, 1, :], b2_done)

            def up(layer, i, par, e, pair):
                if layer == 0 and (e or pair or not i.first):
                    pe.wait_ge(act_done.sem, act_done.at(layer, i, 2 * e + pair))
                elif layer == 1 and e:
                    pe.wait_ge(act_done.sem, act_done.at(layer, i, 2 * (e - 1) + pair + 1))
                for ft in (2 * pair, 2 * pair + 1):
                    last = pe.matmul(up_banks[layer][pair][:, (ft % 2) * L:(ft % 2 + 1) * L],
                                     w1[:, e, ft * P:(ft + 1) * P], hidT[:, par, :], start=True, stop=True)
                last.then_inc(up_done.sem, 1)

            def down(layer, i, e, t, part=(0, FT)):
                if t == 0 and part[0] == 0:
                    pe.wait_ge(act_done.sem, act_done.at(layer, i, 2 * e + 2))
                    open_bank(down_read)
                for ft in range(*part):
                    last = pe.matmul(p7[:, t * D:(t + 1) * D], hT[:, e % 2, ft, t * P:(t + 1) * P],
                                     w2[:, e, ft, :], start=ft == 0, stop=ft == FT - 1)
                if t == T - 1 and part[1] == FT:
                    last.then_inc(down_done.sem, 1)

            def iteration(layer, it, par, F_, A_, N_):
                f, b, nx, odd = it, it + 1, it + 2, 1 - par
                pe_layer[0] = layer
                if layer == 1 and not A_ and not F_:
                    pe.wait_ge(loaded1, counts[loaded1])
                if layer == 0 and A_ and not F_:
                    pe.wait_ge(shifts_loaded, 16 * (1 + RHO))
                if A_ and not F_:
                    pe.wait_ge((weights0, weights1)[layer], counts[(weights0, weights1)[layer]])
                tail = [(f, par, layer, UNITS - 2), (f, par, layer, UNITS - 1)] if F_ else []
                only = F_ and not A_
                for s in range(G):
                    def more(x):
                        extra(layer, s, x, f, b, nx, par, F_, A_, N_)

                    n, g = pairs_of(layer, s)[0]
                    u = T * g
                    if F_ and layer == 0:
                        up(layer, f, par, 2 * s, 0)
                    if A_:
                        scores(layer, b, odd, n, u)
                    if layer == 1 and tail:
                        values(layer, *tail[0], only)
                    more(0)
                    if F_:
                        up(layer, f, par, 2 * s, 1)
                    if layer == 0:
                        if tail:
                            values(layer, *tail[0], only)
                        more(1)
                        if A_:
                            scores(layer, b, odd, n, u + 1, (0,))
                        if tail:
                            turn_values(layer, *tail[0])
                        if A_:
                            scores(layer, b, odd, n, u + 1, (1,))
                            turn_max(layer, b, n, u)
                        if F_:
                            up(layer, f, par, 2 * s + 1, 0)
                        if tail:
                            values(layer, *tail[1], only)
                        more(2)
                        if A_:
                            subtract(layer, b, n, u)
                        if tail:
                            turn_values(layer, *tail[1])
                        more(3)
                        if F_:
                            up(layer, f, par, 2 * s + 1, 1)
                        if A_:
                            turn_max(layer, b, n, u + 1)
                        if F_:
                            down(layer, f, 2 * s, 0)
                            down(layer, f, 2 * s, 1)
                        if A_:
                            subtract(layer, b, n, u + 1)
                        more(4)
                        if F_:
                            down(layer, f, 2 * s + 1, 0)
                            down(layer, f, 2 * s + 1, 1)
                        more(5)
                        more(6)
                        tail = [(b, odd, n, u), (b, odd, n, u + 1)] if A_ else []
                        continue
                    if tail:
                        turn_values(layer, *tail[0])
                    if A_:
                        scores(layer, b, odd, n, u + 1)
                        turn_max(layer, b, n, u)
                    if F_:
                        up(layer, f, par, 2 * s + 1, 0)
                    more(1)
                    if tail:
                        values(layer, *tail[1], only)
                    if F_:
                        up(layer, f, par, 2 * s + 1, 1)
                    if tail:
                        turn_values(layer, *tail[1])
                    if A_:
                        subtract(layer, b, n, u)
                        turn_max(layer, b, n, u + 1)
                    if F_:
                        down(layer, f, 2 * s, 0)
                        down(layer, f, 2 * s, 1)
                    if A_:
                        subtract(layer, b, n, u + 1)
                    more(2)
                    tail = []
                    if A_:
                        tail = [(b, odd, n, u), (b, odd, n, u + 1)]
                        n, g = pairs_of(layer, s)[1]
                        u = T * g
                        scores(layer, b, odd, n, u)
                    more(3)
                    if A_:
                        values(layer, *tail[0], False)
                    if F_:
                        down(layer, f, 2 * s + 1, 0)
                    if A_:
                        turn_values(layer, *tail[0])
                        scores(layer, b, odd, n, u + 1)
                        turn_max(layer, b, n, u)
                    if F_:
                        down(layer, f, 2 * s + 1, 1, (0, FT // 2))
                    if A_:
                        values(layer, *tail[1], False)
                        subtract(layer, b, n, u)
                        turn_values(layer, *tail[1])
                    if F_:
                        down(layer, f, 2 * s + 1, 1, (FT // 2, FT))
                    if A_:
                        turn_max(layer, b, n, u + 1)
                        tail = [(b, odd, n, u), (b, odd, n, u + 1)]
                    if F_ and s < G - 1:
                        up(layer, f, par, 2 * s + 2, 0)
                    elif A_ and s == G - 1:
                        up(layer, b, odd, 0, 0)
                    if A_:
                        subtract(layer, b, n, u + 1)
                    more(4)
                    more(5)
                    more(6)

            run(pe, list(reads.values()), iteration)

        @block.vector
        def _(v):
            v.wait_ge(shifts_loaded, 16)
            v.memset(ext[:, 0:192], 0.0)
            v.memset(ext[:, 192 + NPOS:512], 0.0).then_inc(dve.sem, 1)
            steps = Tally(LOOP_STEPS[:])
            roots = Tally(LOOP_ROOTS[:])
            v.wait_ge(dve.sem, steps.next())
            v.tensor_scalar(ext[:, 0:192], ext[:, 0:192], ext[:, 192:193], None, ALU.add).then_inc(ext_ready, 1)
            v.tensor_scalar(ext[:, 192 + NPOS:512], ext[:, 192 + NPOS:512], ext[:, 191 + NPOS:192 + NPOS], None,
                            ALU.add).then_inc(ext_ready, 1)
            v.wait_ge(loaded, counts[loaded])
            v.wait_ge(ready, 5)
            def link(ins):
                ins.then_inc(dve.sem, 1)
                v.wait_ge(dve.sem, steps.next())

            def close():
                v.sem_inc(small_read.sem, 1)

            def held(layer, c=D):
                return small[layer][:, 0:T * c].rearrange("p (t d) -> p t d", t=T)

            def plus(dst, x_, y_):
                link(v.tensor_tensor(dst, x_, y_, ALU.add))

            def spread_of(src, eps):
                for t in range(T):
                    v.bn_stats(stats[:, t, :], src[t])
                v.drain()
                for t in range(T):
                    last = v.bn_aggr(mv[:, t, :], stats[:, t, :])
                link(last)
                v.tensor_scalar(ve[:, :], mv[:, :, 1], eps, None, ALU.add).then_inc(var_ready.sem, 1)

            def norm(src, dst):
                v.wait_ge(rstd_ready.sem, roots.next())
                for t in range(T):
                    last = v.tensor_scalar(dst[:, t, :], src[t], mv[:, t, 0:1], rstd[:, t:t + 1], ALU.subtract, ALU.mult)
                return last

            def take_v(layer, i, par, n):
                _, set_ = attention(layer, par, n)
                v.wait_ge(v_proj.sem, v_proj.at(layer, i, n + 1))
                for t in range(T):
                    dst = vp[:, set_, t, :, 0:HD]
                    src = small[layer][:, t * D:(t + 1) * D].rearrange("p (h d) -> p h d", d=HD)
                    bv = rows[:, ROWS.index(f"{ATTN[layer]}_bv"), :].rearrange("p (h d) -> p h d", d=HD)
                    last = v.tensor_tensor(dst, src, bv, ALU.add)
                last.then_inc(v_ready.sem, 1)
                v.wait_ge(v_ready.sem, v_ready.at(layer, i, n + 1))
                close()

            def far_keys(i, par):
                v.wait_ge(k_taken.sem, k_taken.at(0, i, 2))
                for t in range(T):
                    last = v.tensor_scalar(far_full[0:96, :, t * P:(t + 1) * P], k_full[0:96, :, t * P:(t + 1) * P],
                                           far[0:96, t:t + 1], None, ALU.add)
                link(last)
                v.tensor_copy(ksa[0:96, par, :, :], far_full[0:96, :, :]).then_inc(far_taken.sem, 1)

            def mask_spread(layer, i, g, pair):
                v.wait_ge(qx_proj.sem, qx_proj.at(layer, i, 2 * g + pair + 1))
                v.tensor_tensor(qx[:, g % 2, 2 * pair:2 * pair + 2, :], small[0][:, :].rearrange("p (h l) -> p h l", h=2),
                                rmask.unsqueeze(1).broadcast_to((P, 2, L)), ALU.mult).then_inc(qx_out.sem, 1)
                v.wait_ge(qx_out.sem, qx_out.at(layer, i, 2 * g + pair + 1))
                close()

            def partial_max(layer, i, n, u):
                v.wait_ge(scores_ready.sem, scores_ready.at(layer, i, n * UNITS + u + 1))
                link(v.tensor_reduce(pm[:, :], score[u % 2][:, :].rearrange("p (b c) -> p b c", c=32), AX.X, ALU.max,
                                     apply_transpose=True))
                v.tensor_tensor(pm2[:, u % 2, :], pm[:, 0:16], pm[:, 16:32], ALU.max).then_inc(part_max.sem, 1)

            def minus_max(layer, i, n, u):
                v.wait_ge(max_turned.sem, max_turned.at(layer, i, n * UNITS + u + 1))
                v.tensor_reduce(nm[:, u % 2, :], p6[0:16, 256:256 + P].rearrange("p (q m) -> p m q", q=4), AX.X, ALU.max,
                                negate=True).then_inc(nm_ready.sem, 1)
                v.wait_ge(nm_ready.sem, nm_ready.at(layer, i, n * UNITS + u + 1))
                v.tensor_tensor(shift[:, u % 2, :, :], nm[:, u % 2, :].unsqueeze(1).broadcast_to((16, 16, 32)),
                                const[0:16, EYE16:EYE16 + 16].unsqueeze(2).broadcast_to((16, 16, 32)),
                                ALU.mult).then_inc(shift_rows.sem, 1)

            def divide(layer, i, par, n, u):
                g, half_ = divmod(u, T)
                v.wait_ge(pv_turned.sem, pv_turned.at(layer, i, n * UNITS + u + 1))
                src = p6[:, P:2 * P].rearrange("p (h c) -> p h c", h=GH)
                link(v.reciprocal(rden[:, :], src[:, :, HD]))
                dst = ao[:, par if layer == 0 else n, half_, g * 32:(g + 1) * 32].rearrange("p (h d) -> p h d", d=HD)
                v.tensor_tensor(dst, src[:, :, 0:HD], rden[:, :].unsqueeze(2).broadcast_to((P, GH, HD)),
                                ALU.mult).then_inc(divided.sem, 1)

            def take_logits(layer, i):
                v.wait_ge(logits_done.sem, logits_done.at(layer, i, 1))
                src = held(layer, E)
                link(v.tensor_reduce(red[:, :], src, AX.X, ALU.max))
                link(v.tensor_tensor(logit[:, :, :], src, red[:, :].unsqueeze(2).broadcast_to((P, T, E)), ALU.subtract))
                close()
                v.sem_inc(centred.sem, 1)

            def router_softmax(layer, i):
                v.wait_ge(exps_done.sem, exps_done.at(layer, i, 1))
                link(v.tensor_reduce(red[:, :], prob[:, :, :], AX.X, ALU.add))
                link(v.reciprocal(red2[:, :], red[:, :]))
                link(v.tensor_tensor(prob[:, :, :], prob[:, :, :], red2[:, :].unsqueeze(2).broadcast_to((P, T, E)), ALU.mult))
                if layer == 1:
                    link(v.tensor_reduce(red[:, :], prob[:, :, :], AX.X, ALU.max))
                    v.tensor_tensor(logit[:, :, :], prob[:, :, :], red[:, :].unsqueeze(2).broadcast_to((P, T, E)),
                                    ALU.subtract).then_inc(centred.sem, 1)

            def compare():
                for t in range(T):
                    other = prob[:, t, :].unsqueeze(1).broadcast_to((P, E, E))
                    own = prob[:, t, :].unsqueeze(2).broadcast_to((P, E, E))
                    v.tensor_tensor(cmp[:, t, :, :], other, own, ALU.is_gt)
                    last = v.tensor_tensor(cmp2[:, t, :, :], other, own, ALU.is_equal)
                link(last)
                lower = const[:, LOWER:LOWER + E * E].unsqueeze(1).broadcast_to((P, T, E * E))
                flat, flat2 = (c[:, :, :, :].rearrange("p t e j -> p t (e j)") for c in (cmp, cmp2))
                link(v.tensor_tensor(flat2, flat2, lower, ALU.mult))
                plus(flat, flat, flat2)

            def choose(layer, i, par):
                link(v.tensor_reduce(sel[:, :, :], cmp[:, :, :, :], AX.X, ALU.add))
                link(v.tensor_scalar(sel[:, :, :], sel[:, :, :], 1.5, None, ALU.is_lt))
                if layer == 0:
                    v.tensor_tensor(gate[:, par], prob[:, :, :], sel[:, :, :], ALU.mult).then_inc(gates_ready.sem, 1)
                else:
                    v.wait_ge(exps_done.sem, exps_done.at(layer, i, 2))
                    link(v.tensor_tensor(gate[:, par], eprob[:, :, :], sel[:, :, :], ALU.mult))
                    link(v.tensor_reduce(red[:, :], gate[:, par], AX.X, ALU.add))
                    link(v.reciprocal(red2[:, :], red[:, :]))
                    v.tensor_tensor(gate[:, par], gate[:, par], red2[:, :].unsqueeze(2).broadcast_to((P, T, E)),
                                    ALU.mult).then_inc(gates_ready.sem, 1)
                v.wait_ge(gates_ready.sem, gates_ready.at(layer, i, 1))

            def add_expert(layer, i, par, e, sums):
                v.wait_ge(down_done.sem, down_done.at(layer, i, e + 1))
                for t in range(T):
                    last = v.scalar_tensor_tensor(sums[:, par, t, :], p7[:, t * D:(t + 1) * D], gate[:, par, t, e:e + 1],
                                                  sums[:, par, t, :], ALU.mult, ALU.add)
                link(last)
                v.sem_inc(down_read.sem, 1)

            def add_product(done, layer, i, k, dst, other):
                v.wait_ge(done.sem, done.at(layer, i, k))
                plus(dst, other, held(layer))
                close()

            def batch(i):
                return X[:, bass.ds(i.times(T), T), :]

            def tiles_of(i):
                return [X[:, bass.ds(i.times(T, t), 1), :].rearrange("p t d -> p (t d)") for t in range(T)]

            def tiles(x_):
                return [x_[:, t, :] for t in range(T)]

            def extra(layer, s, x, f, b, nx, par, F_, A_, N_):
                at = (layer, s, x)
                odd = 1 - par
                if layer == 0:
                    if A_ and s < G - 1 and x < 2:
                        mask_spread(0, b, s + 1, x)
                    if A_ and at == (0, 0, 4):
                        spread_of(tiles(xn[:, odd]), 1e-5)
                    if A_ and at == (0, 0, 5):
                        norm(tiles(xn[:, odd]), n1).then_inc(normed.sem, 1)
                    if F_ and at == (0, 0, 4):
                        add_product(o_proj, 0, f, 1, res[:, par], res[:, par])
                    if A_ and at == (0, 0, 5):
                        plus(res[:, odd], batch(b), row("L0_attn_bo"))
                        plus(xn[:, odd], xn[:, odd], row("L0_ffn_mix_b"))
                    if A_ and at == (0, 1, 3):
                        add_product(mix_done, 0, b, 1, x1[:, :, :], n1[:, :, :])
                    if A_ and at == (0, 1, 4):
                        plus(x1[:, :, :], x1[:, :, :], xn[:, odd])
                        spread_of(tiles(x1), 1e-5)
                    if A_ and at == (0, 1, 5):
                        norm(tiles(x1), n1).then_inc(normed.sem, 1)
                    if A_ and at == (0, 1, 5):
                        plus(res[:, odd], res[:, odd], x1[:, :, :])
                    if A_ and at == (0, 2, 3):
                        take_logits(0, b)
                    if N_ and at == (0, 0, 6):
                        spread_of(tiles_of(nx), 1e-5)
                    if N_ and at == (0, 1, 0):
                        norm(tiles_of(nx), xn[:, par]).then_inc(xn_ready.sem, 1)
                    if A_ and at == (0, 2, 5):
                        router_softmax(0, b)
                    if A_ and at == (0, 2, 6):
                        compare()
                        choose(0, b, odd)
                    if A_ and at == (0, 3, 4):
                        add_product(b2_done, 0, b, 1, res[:, odd], res[:, odd])
                    if N_ and at == (0, 3, 1):
                        take_v(0, nx, par, 0)
                    if N_ and at == (0, 3, 3):
                        mask_spread(0, nx, 0, 0)
                    if N_ and at == (0, 3, 7):
                        far_keys(nx, par)
                    if N_ and at == (0, 3, 5):
                        mask_spread(0, nx, 0, 1)
                    if F_ and at == (0, 3, 6):
                        link(v.tensor_scalar(batch(f), res[:, par], 1.0, None, ALU.mult))
                    return
                if A_ and at == (1, 1, 1):
                    take_v(1, b, odd, 1)
                if F_ and at == (1, 0, 3):
                    add_product(o_proj, 1, f, 2, res[:, par], res[:, par])
                if F_ and at == (1, 1, 5):
                    plus(res[:, par], res[:, par], row("L1_ffn_ln2_b"))
                if A_ and at == (1, 0, 5):
                    plus(res[:, odd], batch(b), row("L1_attn_bo"))
                    plus(x1[:, :, :], xn[:, odd], row("L1_ffn_bo"))
                if N_ and at == (1, 0, 6):
                    spread_of(tiles_of(nx), 1e-5)
                if N_ and at == (1, 1, 0):
                    norm(tiles_of(nx), xn[:, par]).then_inc(xn_ready.sem, 1)
                if A_ and at == (1, 2, 3):
                    add_product(o_proj, 1, b, 1, x1[:, :, :], x1[:, :, :])
                if A_ and at == (1, 2, 4):
                    spread_of(tiles(x1), 1e-6)
                if A_ and at == (1, 2, 5):
                    norm(tiles(x1), acc[:, odd]).then_inc(normed.sem, 1)
                if A_ and at == (1, 3, 2):
                    take_logits(1, b)
                if A_ and at == (1, 3, 4):
                    router_softmax(1, b)
                if F_ and at == (1, 3, 4):
                    spread_of(tiles(acc[:, par]), 1e-6)
                if A_ and at == (1, 3, 5):
                    compare()
                if F_ and at == (1, 0, 7):
                    choose(1, f, par)
                if F_ and at == (1, 1, 6):
                    add_product(b2_done, 1, f, 1, acc[:, par], acc[:, par])
                if F_ and at == (1, 3, 6):
                    link(norm(tiles(acc[:, par]), n1))
                    link(v.tensor_tensor(n1[:, :, :], n1[:, :, :], row("L1_ffn_ln2_g"), ALU.mult))
                    v.tensor_tensor(batch(f), res[:, par], n1[:, :, :], ALU.add).then_inc(out_ready.sem, 1)
                    v.wait_ge(out_ready.sem, out_ready.at(1, f, 1))

            def iteration(layer, it, par, F_, A_, N_):
                f, b, nx, odd = it, it + 1, it + 2, 1 - par
                sums = res if layer == 0 else acc
                if layer == 0 and A_ and not F_:
                    v.wait_ge(x_loaded, counts[x_loaded])
                if layer == 1 and not A_ and not F_:
                    v.wait_ge(loaded1, counts[loaded1])
                tail = [(f, par, layer, UNITS - 2), (f, par, layer, UNITS - 1)] if F_ else []
                for s in range(G):
                    def more(x):
                        extra(layer, s, x, f, b, nx, par, F_, A_, N_)

                    n, g = pairs_of(layer, s)[0]
                    u = T * g
                    more(0)
                    if A_:
                        partial_max(layer, b, n, u)
                    if layer == 0:
                        more(1)
                    if tail:
                        divide(layer, *tail[0])
                    if A_:
                        minus_max(layer, b, n, u)
                        partial_max(layer, b, n, u + 1)
                    more(2 if layer == 0 else 1)
                    if tail:
                        divide(layer, *tail[1])
                    if layer == 0:
                        more(3)
                    if A_:
                        minus_max(layer, b, n, u + 1)
                        tail = [(b, odd, n, u), (b, odd, n, u + 1)]
                    else:
                        tail = []
                    more(7)
                    if F_:
                        add_expert(layer, f, par, 2 * s, sums)
                    if layer == 1:
                        more(2)
                        n, g = pairs_of(layer, s)[1]
                        u = T * g
                        more(3)
                        if A_:
                            partial_max(layer, b, n, u)
                            divide(layer, *tail[0])
                            minus_max(layer, b, n, u)
                            partial_max(layer, b, n, u + 1)
                            divide(layer, *tail[1])
                            minus_max(layer, b, n, u + 1)
                            tail = [(b, odd, n, u), (b, odd, n, u + 1)]
                        if F_:
                            add_expert(layer, f, par, 2 * s + 1, sums)
                        more(4)
                    else:
                        more(4)
                        if F_:
                            add_expert(layer, f, par, 2 * s + 1, sums)
                    more(5)
                    more(6)

            run(v, [steps, roots], iteration)


LOOP_STEPS = [92, 130]
LOOP_ROOTS = [6, 6]
LOOP_SMALL = [44, 38]
LOOP_DOWN = [16, 16]

WEIGHTS_T = ["Wq", "Wk", "Wv", "Wo"]


def constants():
    import numpy as np
    c = np.zeros((P, NCONST), np.float32)
    p = np.arange(P)[:, None]
    c[:, EYE:EYE + P] = np.eye(P)
    c[:, RMASK:RMASK + L] = (np.arange(L)[None, :] % RHO) == p // HD
    c[:, HMASK:HMASK + GH] = (p % 32) // HD == np.arange(GH)[None, :]
    c[:16, EYE16:EYE16 + 16] = np.eye(16)
    c[:, LOWER:SPREAD] = (np.arange(E)[None, :] < np.arange(E)[:, None]).reshape(-1)
    row, col = p % 32, np.arange(P)[None, :] % HD
    for s in range(GH):
        c[:64, SPREAD + s * P:SPREAD + (s + 1) * P] = (row == s * HD + col)[:64]
    return c


def kernel(**inputs):
    import numpy as np
    import concourse.bacc as bacc
    from concourse.bass_utils import run_bass_kernel_spmd

    nc = bacc.Bacc("TRN2", target_bir_lowering=False, num_devices=1)
    arrays = {"const": constants(), "rows": np.stack([np.asarray(inputs[n]) for n in ROWS])}
    arrays["far"] = np.tile(np.asarray(inputs["L0_attn_dist_emb"])[[0, NPOS - 1]].T, (P // HD, 1))
    for name, value in inputs.items():
        value = np.asarray(value)
        if name in ROWS:
            continue
        if name[:7] in ("L0_attn", "L1_attn") and name[8:] in WEIGHTS_T or name == "L0_attn_dist_emb":
            value = value.T
        if name.split("_")[-1] in ("Wq", "Wk"):
            value = np.tile(value.reshape(P, G, 1, D // G), (1, 1, GH, 1)).reshape(P, G * P)
        if name[8:] in ("bq", "bk"):
            value = np.tile(value.reshape(G, D // G).T, (GH, 1))
        if name in ("L0_ffn_b1", "L1_ffn_be1"):
            value = value.reshape(E * FT, P).T
        arrays[name] = np.ascontiguousarray(value)
    a = {n: nc.dram_tensor(f"in_{n}", v.shape, mybir.dt.from_np(v.dtype), kind="ExternalInput").ap() for n, v in arrays.items()}
    out = nc.dram_tensor("out_0", (B, L, D), mybir.dt.float32, kind="ExternalOutput").ap()
    build(nc, a, out)
    r = run_bass_kernel_spmd(nc, [{f"in_{n}": v for n, v in arrays.items()}], core_ids=[0])
    return r.results[0]["out_0"]
```
